# Optimizing a Trainium2 kernel written in Bass

```python
import numpy as np
import jax
import jax.numpy as jnp

def _softmax(x, axis=-1):
    return jax.nn.softmax(x, axis=axis)

def _gelu(x):
    return jax.nn.gelu(x, approximate=True)

def _silu(x):
    return jax.nn.silu(x)

def _sigmoid(x):
    return jax.nn.sigmoid(x)

def _layernorm(x, axis=-1, eps=1e-05):
    m = jnp.mean(x, axis=axis, keepdims=True)
    v = jnp.var(x, axis=axis, keepdims=True)
    return (x - m) / jnp.sqrt(v + eps)

def _scatter_add(tgt, idx, src, axis=0):
    return tgt.at[idx].add(src)

def _segment_sum(src, seg, n):
    return jax.ops.segment_sum(src, seg, n)
kernel_name = 'mk_recurrent_d1_jaxref_r8_defa77'

def setup_inputs(seed: int=0):
    np.random.seed(seed)
    _w = jnp.asarray

    def _L0_attn_setup():
        import jax, jax.numpy as jnp
        import numpy as np
        NEG_INF = -1e+38

        def _wkv_scan(time_decay, time_first, key, value):
            B, S, D = key.shape
            w = -jnp.exp(time_decay)

            def step(carry, kv):
                num, den, mx = carry
                k, v = kv
                m_out = jnp.maximum(mx, k + time_first)
                e1 = jnp.exp(mx - m_out)
                e2 = jnp.exp(k + time_first - m_out)
                out = (e1 * num + e2 * v) / (e1 * den + e2)
                m_new = jnp.maximum(mx + w, k)
                e1 = jnp.exp(mx + w - m_new)
                e2 = jnp.exp(k - m_new)
                return ((e1 * num + e2 * v, e1 * den + e2, m_new), out)
            init = (jnp.zeros((B, D), jnp.float32), jnp.zeros((B, D), jnp.float32), jnp.full((B, D), NEG_INF, jnp.float32))
            kv = (jnp.moveaxis(key, 1, 0), jnp.moveaxis(value, 1, 0))
            _, out = jax.lax.scan(step, init, kv)
            return jnp.moveaxis(out, 0, 1)
        key = jax.random.key(seed)
        ks = jax.random.split(key, 10)
        B, S, H = (4, 256, 256)
        D = H
        return {'hidden': jax.random.normal(ks[0], (B, S, H), jnp.float32), 'time_decay': jax.random.normal(ks[1], (D,), jnp.float32), 'time_first': jax.random.normal(ks[2], (D,), jnp.float32), 'time_mix_key': jax.random.uniform(ks[3], (1, 1, H), jnp.float32), 'time_mix_value': jax.random.uniform(ks[4], (1, 1, H), jnp.float32), 'time_mix_receptance': jax.random.uniform(ks[5], (1, 1, H), jnp.float32), 'Wk': jax.random.normal(ks[6], (D, H), jnp.float32) / np.sqrt(H), 'Wv': jax.random.normal(ks[7], (D, H), jnp.float32) / np.sqrt(H), 'Wr': jax.random.normal(ks[8], (D, H), jnp.float32) / np.sqrt(H), 'Wo': jax.random.normal(ks[9], (H, D), jnp.float32) / np.sqrt(D)}
    _L0_attn_in = _L0_attn_setup()

    def _L0_ffn_setup():
        import jax, jax.numpy as jnp
        import numpy as np
        D_MODEL = 256
        FFN_HIDDEN = 256
        N_EXPERTS = 16
        TOP_K = 4
        key = jax.random.key(seed)
        k1, k2, k3, k4, k5 = jax.random.split(key, 5)
        scale = 1.0 / np.sqrt(D_MODEL)
        x = jax.random.normal(k1, (2, 512, D_MODEL), dtype=jnp.float32)
        w_router = jax.random.normal(k2, (N_EXPERTS, D_MODEL), dtype=jnp.float32) * scale
        w_gate = jax.random.normal(k3, (N_EXPERTS, D_MODEL, FFN_HIDDEN), dtype=jnp.float32) * scale
        w_up = jax.random.normal(k4, (N_EXPERTS, D_MODEL, FFN_HIDDEN), dtype=jnp.float32) * scale
        w_down = jax.random.normal(k5, (N_EXPERTS, FFN_HIDDEN, D_MODEL), dtype=jnp.float32) * (1.0 / np.sqrt(FFN_HIDDEN))
        return {'x': x, 'w_router': w_router, 'w_gate': w_gate, 'w_up': w_up, 'w_down': w_down}
    _L0_ffn_in = _L0_ffn_setup()
    _d = {'L0_attn_hidden': _L0_attn_in['hidden'], 'L0_attn_time_decay': _L0_attn_in['time_decay'], 'L0_attn_time_first': _L0_attn_in['time_first'], 'L0_attn_time_mix_key': _L0_attn_in['time_mix_key'], 'L0_attn_time_mix_value': _L0_attn_in['time_mix_value'], 'L0_attn_time_mix_receptance': _L0_attn_in['time_mix_receptance'], 'L0_attn_Wk': _L0_attn_in['Wk'], 'L0_attn_Wv': _L0_attn_in['Wv'], 'L0_attn_Wr': _L0_attn_in['Wr'], 'L0_attn_Wo': _L0_attn_in['Wo'], 'L0_ffn_w_router': _L0_ffn_in['w_router'], 'L0_ffn_w_gate': _L0_ffn_in['w_gate'], 'L0_ffn_w_up': _L0_ffn_in['w_up'], 'L0_ffn_w_down': _L0_ffn_in['w_down']}
    _x0 = _d['L0_attn_hidden']
    _d['L0_attn_hidden'] = jax.random.normal(jax.random.fold_in(jax.random.key(seed), 1), (4, 512, 256), dtype=_x0.dtype)
    del _x0
    return _d

def reference(L0_attn_hidden, L0_attn_time_decay, L0_attn_time_first, L0_attn_time_mix_key, L0_attn_time_mix_value, L0_attn_time_mix_receptance, L0_attn_Wk, L0_attn_Wv, L0_attn_Wr, L0_attn_Wo, L0_ffn_w_router, L0_ffn_w_gate, L0_ffn_w_up, L0_ffn_w_down):

    def _L0_attn_ref(hidden, time_decay, time_first, time_mix_key, time_mix_value, time_mix_receptance, Wk, Wv, Wr, Wo):
        import jax, jax.numpy as jnp
        import numpy as np
        NEG_INF = -1e+38

        def _wkv_scan(time_decay, time_first, key, value):
            B, S, D = key.shape
            w = -jnp.exp(time_decay)

            def step(carry, kv):
                num, den, mx = carry
                k, v = kv
                m_out = jnp.maximum(mx, k + time_first)
                e1 = jnp.exp(mx - m_out)
                e2 = jnp.exp(k + time_first - m_out)
                out = (e1 * num + e2 * v) / (e1 * den + e2)
                m_new = jnp.maximum(mx + w, k)
                e1 = jnp.exp(mx + w - m_new)
                e2 = jnp.exp(k - m_new)
                return ((e1 * num + e2 * v, e1 * den + e2, m_new), out)
            init = (jnp.zeros((B, D), jnp.float32), jnp.zeros((B, D), jnp.float32), jnp.full((B, D), NEG_INF, jnp.float32))
            kv = (jnp.moveaxis(key, 1, 0), jnp.moveaxis(value, 1, 0))
            _, out = jax.lax.scan(step, init, kv)
            return jnp.moveaxis(out, 0, 1)
        shifted = jnp.pad(hidden, ((0, 0), (1, 0), (0, 0)))[:, :-1]
        xk = hidden * time_mix_key + shifted * (1.0 - time_mix_key)
        xv = hidden * time_mix_value + shifted * (1.0 - time_mix_value)
        xr = hidden * time_mix_receptance + shifted * (1.0 - time_mix_receptance)
        k = jnp.einsum('bsh,dh->bsd', xk, Wk)
        v = jnp.einsum('bsh,dh->bsd', xv, Wv)
        r = jax.nn.sigmoid(jnp.einsum('bsh,dh->bsd', xr, Wr))
        rwkv = _wkv_scan(time_decay, time_first, k, v)
        return jnp.einsum('bsd,hd->bsh', r * rwkv, Wo)

    def _L0_ffn_ref(x, w_router, w_gate, w_up, w_down):
        import jax, jax.numpy as jnp
        import numpy as np
        D_MODEL = 256
        FFN_HIDDEN = 256
        N_EXPERTS = 16
        TOP_K = 4
        B, S, D = x.shape
        xt = x.reshape(-1, D)
        logits = jnp.einsum('td,ed->te', xt, w_router)
        probs = jax.nn.softmax(logits, axis=-1)
        top_w, top_e = jax.lax.top_k(probs, TOP_K)
        top_w = top_w / jnp.sum(jnp.abs(top_w), axis=-1, keepdims=True)
        out = jnp.zeros_like(xt)
        for e in range(N_EXPERTS):
            coeff = jnp.sum(jnp.where(top_e == e, top_w, 0.0), axis=-1)
            h = jax.nn.silu(xt @ w_gate[e]) * (xt @ w_up[e])
            out = out + coeff[:, None] * (h @ w_down[e])
        return out.reshape(B, S, D)
    x = L0_attn_hidden
    xn = _layernorm(x, axis=-1)
    s = _L0_attn_ref(xn, L0_attn_time_decay, L0_attn_time_first, L0_attn_time_mix_key, L0_attn_time_mix_value, L0_attn_time_mix_receptance, L0_attn_Wk, L0_attn_Wv, L0_attn_Wr, L0_attn_Wo)
    g = _silu(_L0_ffn_ref(xn, L0_ffn_w_router, L0_ffn_w_gate, L0_ffn_w_up, L0_ffn_w_down))
    x = x + s * g
    return x

_drawn_inputs = setup_inputs


def setup_inputs(seed=0):
    import zlib

    import numpy as np

    out = dict(_drawn_inputs(seed))
    spreads = {}
    factors = {'L0_attn_time_decay': 3.284,
     'L0_attn_time_first': 3.693,
     'L0_attn_time_mix_key': 5.44,
     'L0_attn_time_mix_value': 3.047,
     'L0_attn_time_mix_receptance': 6.339,
     'L0_attn_Wk': 3.254,
     'L0_attn_Wr': 3.259}
    for name, (base, spread) in spreads.items():
        noise = np.random.default_rng([zlib.crc32(name.encode()), seed]).standard_normal(out[name].shape)
        drawn = base * np.exp(spread * noise) if base else spread * noise
        out[name] = jnp.asarray(drawn.astype(out[name].dtype))
    for name, factor in factors.items():
        out[name] = (out[name] * factor).astype(out[name].dtype)
    return out
```

```python
import concourse.bass as bass
from concourse import mybir
from contextlib import ExitStack

BATCH, SEQ, D = 4, 512, 256
E, TOPK = 16, 4
P = 128
C = D // P
TOK = BATCH * SEQ
T = TOK // P
TB = SEQ // P
ROWS = TOK * TOPK
OUTER = 4
PAIRS = -(-(ROWS // P + E - 1) // (2 * OUTER))
NP = OUTER * PAIRS
NT = 2 * NP
HALF = PAIRS // C
LN_EPS = 1e-5
NEG_INF = -1e38
assert PAIRS % 2 == 0 and HALF == 5 and C == 2


def rwkv_times_moe(nc, x_in, vec_in, wkT_in, wvT_in, wrT_in, woT_in, wrouT_in, wg_in, wu_in, wd_in, out):
    f32, i32 = mybir.dt.float32, mybir.dt.int32
    ALU = mybir.AluOpType
    ACT = mybir.ActivationFunctionType
    X = mybir.AxisListType.X

    xn_rows = nc.dram_tensor("xn_rows", [TOK, D], f32, kind="Internal").ap()
    y_rows = nc.dram_tensor("y_rows", [ROWS, D], f32, kind="Internal").ap()

    x_v = x_in.rearrange("b (t p) d -> p b t d", p=P)
    out_v = out.rearrange("b (t p) d -> p (b t) d", p=P)
    xn_v = xn_rows.rearrange("(b t p) d -> p b t d", p=P, t=TB)
    y_v = y_rows.rearrange("(s t p) d -> p t s d", p=P, t=T)

    ctx = ExitStack()
    with ctx:
        def sb(name, shape, dt=f32):
            return ctx.enter_context(nc.sbuf_tensor(name, shape, dt))

        def sem(name):
            return ctx.enter_context(nc.semaphore(name))

        wbig = sb("wbig", [P, 3 * C * E * D])
        wgu = wbig[:, 0:2 * C * E * D].rearrange("p (c e n) -> p c e n", c=C, e=E)
        wdn = wbig[:, 2 * C * E * D:].rearrange("p (c e n) -> p c e n", c=C, e=E)
        kT = sb("kT", [P, C, TOK])
        vT = sb("vT", [P, C, TOK])
        rT = sb("rT", [P, C, TOK])
        woT = sb("woT", [P, C, D])
        ident = sb("ident", [P, P])
        vec = sb("vec", [P, 5 * C])
        decay = sb("decay", [P, C])
        tok_idx = sb("tok_idx", [P, NT], i32)
        dst_idx = sb("dst_idx", [P, NT], i32)
        tile_expert = sb("tile_expert", [1, NT], i32)
        coef4 = sb("coef4", [P, T, TOPK])
        xg = sb("xg", [P, 2, 2, D])
        g_idx = sb("g_idx", [P, 2 * PAIRS], i32)
        s_idx = sb("s_idx", [P, 2 * PAIRS], i32)

        XNT = C * BATCH * (SEQ + 1)
        MIXN = C * SEQ
        arena = sb("arena", [P, XNT + 4 * MIXN + 3 * C * D])
        at = [0]

        def carve(n):
            at[0] += n
            return arena[:, at[0] - n:at[0]]

        xnT = carve(XNT).rearrange("p (c b s) -> p c b s", c=C, b=BATCH)
        diff = carve(MIXN).rearrange("p (c s) -> p c s", c=C)
        mix = [carve(MIXN).rearrange("p (c s) -> p c s", c=C) for _ in range(3)]
        wT = [carve(C * D).rearrange("p (c n) -> p c n", c=C) for _ in range(3)]
        at[0] = 0
        xTg = carve(2 * 2 * D).rearrange("p (b j c t) -> p b j c t", b=2, j=2, c=C)
        sg = carve(2 * 2 * D).rearrange("p (b j n) -> p b j n", b=2, j=2)
        hid = carve(2 * 2 * D).rearrange("p (b j n) -> p b j n", b=2, j=2)
        hT = carve(2 * 2 * D).rearrange("p (b j c t) -> p b j c t", b=2, j=2, c=C)
        ysb = carve(2 * 2 * D).rearrange("p (b j n) -> p b j n", b=2, j=2)
        mrun = carve(SEQ + 1)
        num = carve(SEQ + 1)
        den = carve(SEQ + 1)
        args = carve(4 * SEQ).rearrange("p (a s) -> p a s", a=4)
        ta = carve(SEQ)
        tb = carve(SEQ)
        wrou = sb("wrou", [P, C, E])
        x_sb = rT[:, :, :].rearrange("p c (t n) -> p (c t) n", n=D)

        scr_at = [2 * C * E * D]

        def scratch(*shape):
            n = 1
            for s in shape:
                n *= s
            v = wbig[:, scr_at[0]:scr_at[0] + n]
            scr_at[0] += n
            assert scr_at[0] <= 3 * C * E * D
            if len(shape) == 1:
                return v
            names = "abc"[:len(shape)]
            return v.rearrange(f"p ({' '.join(names)}) -> p {' '.join(names)}", **dict(zip(names, shape)))

        stats = scratch(T, 6)
        mv = scratch(T, 2)
        veps = scratch(T)
        rstd = scratch(T)
        mhalf = scratch(TB)
        rmax, rsum, rinv, cgt, wsum, winv = (scratch(T) for _ in range(6))
        z, prob, gt, eq, pre, sel, wsel, coef, slot, keep = (scratch(T, E) for _ in range(10))
        totT, incl, excl, cmp = (scratch(E, T) for _ in range(4))
        pos = scratch(T, E)
        ntile, tend, tstart, ones16 = (scratch(E) for _ in range(4))
        m8 = scratch(T, 8)
        eqs_prod = scratch(2 * T * TOPK * E)
        eqs = eqs_prod[:, 0:T * TOPK * E].rearrange("p (t n) -> p t n", t=T)
        prod = eqs_prod[:, T * TOPK * E:].rearrange("p (t n) -> p t n", t=T)
        etmp = eqs_prod[:, 0:NT * E].rearrange("p (t e) -> p t e", e=E)
        pos4, ptile, prow, val = (scratch(T, TOPK) for _ in range(4))
        posi = scratch(T * TOPK).bitcast(i32)
        ptilei = scratch(T * TOPK).bitcast(i32)
        prowi = scratch(T * TOPK).bitcast(i32)
        iota_row = scratch(P)
        jrow = scratch(T)
        srow = scratch(TOPK)
        padv = scratch(1)
        upper = scratch(P)
        ones = scratch(P)
        ohA = sb("ohA", [P, 2, TOPK, NT])
        ohB = sb("ohB", [P, 2, TOPK, P])
        padt = scratch(NT)
        esum = scratch(NT)

        y4 = wbig[:, 0:T * TOPK * D].rearrange("p (t s n) -> p t s n", t=T, s=TOPK)
        acc = wbig[:, T * TOPK * D:T * (TOPK + 1) * D].rearrange("p (t n) -> p t n", t=T)
        xre = wbig[:, T * (TOPK + 1) * D:T * (TOPK + 2) * D].rearrange("p (t n) -> p t n", t=T)

        ps = ctx.enter_context(nc.psum_tensor("ps", [P, 8, 512], f32))
        B_XT, B_G, B_HT, B_Y, B_R = 0, 1, 5, 6, 7
        logits = ps[:, B_R, 0:T * E].rearrange("p (t e) -> p t e", t=T)
        prefix = ps[:, B_Y, 0:T * E].rearrange("p (t e) -> p t e", t=T)
        totals = ps[:, B_Y, T * E:2 * T * E].rearrange("p (t e) -> p e t", t=T)
        table = ps[:, B_HT, 0:NT]

        x_in_s = [sem(f"x_in{b}") for b in range(BATCH)]
        small_in = sem("small_in")
        wgu_in, wdn_in = sem("wgu_in"), sem("wdn_in")
        xn_stored = sem("xn_stored")
        consts = sem("consts")
        var_ready, rstd_ready = sem("var_ready"), sem("rstd_ready")
        xn_ready = sem("xn_ready")
        xnt_psum, xnt_ready = sem("xnt_psum"), sem("xnt_ready")
        zcol = sem("zcol")
        diff_ready, mix_ready = sem("diff_ready"), sem("mix_ready")
        decay_ready = sem("decay_ready")
        proj_psum, proj_out = sem("proj_psum"), sem("proj_out")
        logits_ready, z_ready, ez_ready = sem("logits_ready"), sem("z_ready"), sem("ez_ready")
        sel_ready, count_ready = sem("sel_ready"), sem("count_ready")
        digits_ready = sem("digits_ready")
        ohA_ready, ohB_ready, oh_used = sem("ohA_ready"), sem("ohB_ready"), sem("oh_used")
        experts_ready = sem("experts_ready")
        table_ready, index_ready = sem("table_ready"), sem("index_ready")
        pool_turn = sem("pool_turn")
        gi_ready, si_ready = sem("gi_ready"), sem("si_ready")
        xg_in = [sem(f"xg_in{i}") for i in range(2)]
        y_out = [sem(f"y_out{i}") for i in range(2)]
        xt_psum, xt_ready = sem("xt_psum"), sem("xt_ready")
        gu_psum, sg_ready, h_ready = sem("gu_psum"), sem("sg_ready"), sem("h_ready")
        ht_psum, ht_ready = sem("ht_psum"), sem("ht_ready")
        y_psum, y_ready = sem("y_psum"), sem("y_ready")
        args_ready, exps_ready = sem("args_ready"), sem("exps_ready")
        wkv_ready = sem("wkv_ready")
        dve_step, pool_step = sem("dve_step"), sem("pool_step")
        y_in = [sem(f"y_in{i}") for i in range(T // 2)]
        xre_in = sem("xre_in")
        acc_ready, silu_ready, s_psum, ffn_times_s, res_ready = (
            sem("acc_ready"), sem("silu_ready"), sem("s_psum"), sem("ffn_times_s"), sem("res_ready"))
        out_stored = sem("out_stored")

        def wait(eng, s, value):
            if not isinstance(value, int) or value > 0:
                eng.wait_ge(s, value)

        def outer_steps(eng, step):
            step(0)
            with eng.Fori(1, OUTER - 1) as o:
                step(o)
            step(OUTER - 1)

        block = ctx.enter_context(nc.Block())

        @block.sync
        def _(sp):
            for b in range(BATCH):
                sp.dma_start(x_sb[:, b * TB:(b + 1) * TB, :], x_v[:, b]).then_inc(x_in_s[b], 16)
            for dst, src in ((vec[:, :], vec_in), (wrou[:, :, :], wrouT_in.rearrange("(c p) n -> p c n", p=P)),
                             (wT[0], wkT_in.rearrange("(c p) n -> p c n", p=P)),
                             (wT[1], wvT_in.rearrange("(c p) n -> p c n", p=P)),
                             (wT[2], wrT_in.rearrange("(c p) n -> p c n", p=P)),
                             (woT[:, :, :], woT_in.rearrange("(c p) n -> p c n", p=P))):
                sp.dma_start(dst, src).then_inc(small_in, 16)
            for half, src in ((0, wg_in), (1, wu_in)):
                for c in range(C):
                    sp.dma_start(wgu[:, c, :, half * D:(half + 1) * D],
                                 src.rearrange("e (c p) n -> c p e n", p=P)[c]).then_inc(wgu_in, 16)
            sp.wait_ge(index_ready, 1)
            for c in range(C):
                sp.dma_start(wdn[:, c], wd_in.rearrange("e (c p) n -> c p e n", p=P)[c]).then_inc(wdn_in, 16)
            sp.wait_ge(y_psum, NP)
            sp.dma_start(xre, x_in.rearrange("b (t p) d -> p (b t) d", p=P)).then_inc(xre_in, 16)
            for i in range(2):
                sp.wait_ge(y_out[i], 32 * (NP // 2))
            for n in range(T // 2):
                for t in (2 * n, 2 * n + 1):
                    sp.dma_start(y4[:, t], y_v[:, t]).then_inc(y_in[n], 16)
            for n in range(T // 2):
                sp.wait_ge(res_ready, n + 1)
                sp.dma_start(out_v[:, 2 * n:2 * n + 2, :], acc[:, 2 * n:2 * n + 2, :]).then_inc(out_stored, 16)
            sp.wait_ge(out_stored, 16 * (T // 2))

        @block.gpsimd
        def _(pool):
            done = [0]

            def link(ins):
                done[0] += 1
                ins.then_inc(pool_step, 1)
                pool.wait_ge(pool_step, done[0])

            link(pool.memset(ident[:, :], 0.0))
            pool.affine_select(out=ident[:, :], in_=ident[:, :], compare_op=ALU.not_equal, fill=1.0,
                               base=0, pattern=[[-1, P]], channel_multiplier=1).then_inc(consts, 1)
            pool.memset(mhalf, -0.5).then_inc(consts, 1)
            link(pool.memset(keep, 1.0))
            pool.memset(keep[:, :, 0:1], 0.0).then_inc(consts, 1)
            pool.memset(ones, 1.0).then_inc(consts, 1)
            pool.memset(ones16, 1.0).then_inc(consts, 1)
            link(pool.memset(upper, 1.0))
            pool.affine_select(out=upper, in_=upper, compare_op=ALU.is_gt, fill=0.0,
                               base=0, pattern=[[1, P]], channel_multiplier=-1).then_inc(consts, 1)
            for dst, pattern, base, chan in ((iota_row, [[1, P]], 0, 0), (jrow, [[P, T]], 0, 0),
                                             (srow, [[1, TOPK]], 1, 0), (padv, [[1, 1]], ROWS + 1, 1),
                                             (val, [[P, T], [TOK, TOPK]], 1, 1)):
                pool.iota(dst, pattern, base=base, channel_multiplier=chan,
                          allow_small_or_imprecise_dtypes=True).then_inc(consts, 1)
            N_CONSTS = 11
            pool.wait_ge(consts, N_CONSTS)
            for b in range(BATCH):
                t = slice(b * TB, (b + 1) * TB)
                pool.wait_ge(var_ready, b + 1)
                link(pool.tensor_scalar(veps[:, t], mv[:, t, 1], LN_EPS, None, ALU.add))
                pool.tensor_tensor(rstd[:, t], veps[:, t], mhalf, ALU.pow).then_inc(rstd_ready, 1)
            for b in range(BATCH):
                pool.wait_ge(xnt_ready, C * (b + 1))
                if b == 0:
                    pool.wait_ge(zcol, 1)
                else:
                    pool.wait_ge(mix_ready, 3 * b)
                pool.tensor_tensor(diff, xnT[:, :, b, 1:SEQ + 1], xnT[:, :, b, 0:SEQ], ALU.subtract).then_inc(diff_ready, 1)
                if b == 2:
                    pool.wait_ge(digits_ready, 1)
                    for t in range(T):
                        if t >= 2:
                            pool.wait_ge(oh_used, t - 1)
                        for s in range(TOPK):
                            ins = pool.tensor_scalar(ohB[:, t % 2, s], iota_row, prow[:, t, s:s + 1], None, ALU.is_equal)
                        ins.then_inc(ohB_ready, 1)

            LAG = 4
            pool.wait_ge(index_ready, 1)
            for b in range(BATCH):
                pool.wait_ge(xn_stored, 16 * BATCH)

            def wait_alone(s, value):
                wait(pool, s, value)
                if not isinstance(value, int):
                    pool.sem_inc(pool_turn, 1)

            def indices(o, dst, src, landed, ready):
                for par in range(2):
                    wait_alone(landed[par], 16 * PAIRS * o)
                pool.tensor_copy(dst[:, :], src[:, bass.ds(2 * PAIRS * o, 2 * PAIRS)]).then_inc(ready, 1)
                wait_alone(ready, o + 1)

            def gather(o, u):
                par = u % 2
                wait_alone(xt_psum, o * PAIRS + u - 1)
                for j in range(2):
                    n = 2 * u + j
                    pool.indirect_dma_start(out=xg[:, par, j, :], out_offset=None, in_=xn_rows,
                                            in_offset=bass.IndirectOffsetOnAxis(ap=g_idx[:, n:n + 1], axis=0)
                                            ).then_inc(xg_in[par], 16)

            def scatter(o, u):
                par = u % 2
                wait_alone(y_ready, o * PAIRS + u + 1)
                for j in range(2):
                    n = 2 * u + j
                    pool.indirect_dma_start(out=y_rows, in_=ysb[:, par, j, :], in_offset=None,
                                            out_offset=bass.IndirectOffsetOnAxis(ap=s_idx[:, n:n + 1], axis=0),
                                            bounds_check=last_row, oob_is_err=False).then_inc(y_out[par], 16)

            last_row = pool.to_reg(ROWS - 1)

            def step(o):
                indices(o, g_idx, tok_idx, xg_in, gi_ready)
                for u in range(PAIRS):
                    gather(o, u)
                    if u == LAG:
                        indices(o, s_idx, dst_idx, y_out, si_ready)
                    if u >= LAG:
                        scatter(o, u - LAG)
                    elif not isinstance(o, int) or o > 0:
                        scatter(o - 1, u - LAG + PAIRS)

            outer_steps(pool, step)
            for u in range(PAIRS - LAG, PAIRS):
                scatter(OUTER - 1, u)
            pool.wait_ge(xre_in, 16)
            for n in range(T // 2):
                pool.wait_ge(ffn_times_s, n + 1)
                tt = slice(2 * n, 2 * n + 2)
                pool.tensor_tensor(acc[:, tt, :], acc[:, tt, :], xre[:, tt, :], ALU.add).then_inc(res_ready, 1)

        @block.scalar
        def _(act):
            act.wait_ge(small_in, 16 * 6)
            nc.scalar.activation(decay[:, :], vec[:, 0:C], ACT.Exp).then_inc(decay_ready, 1)
            for b in range(BATCH):
                act.wait_ge(xn_ready, b + 1)
                act.dma_start(xn_v[:, b], x_sb[:, b * TB:(b + 1) * TB, :]).then_inc(xn_stored, 16)
                for c in range(C):
                    act.wait_ge(xnt_psum, C * b + c + 1)
                    nc.scalar.copy(xnT[:, c, b, 1:SEQ + 1], ps[:, (B_XT, B_Y)[c], :]).then_inc(xnt_ready, 1)
            act.wait_ge(z_ready, 1)
            nc.scalar.activation(prob, z, ACT.Exp).then_inc(ez_ready, 1)
            for b in range(BATCH):
                for w in range(3):
                    for c in range(C):
                        n = (b * 3 + w) * C + c
                        act.wait_ge(proj_psum, n + 1)
                        dst = (kT, vT, rT)[w][:, c, b * SEQ:(b + 1) * SEQ]
                        src = ps[:, B_G + n % 4, :]
                        if w == 2 and n < 3 * C:
                            act.wait_ge(xn_stored, 16 * BATCH)
                        if w == 2:
                            nc.scalar.activation(dst, src, ACT.Sigmoid).then_inc(proj_out, 1)
                        else:
                            nc.scalar.copy(dst, src).then_inc(proj_out, 1)

            def evac_x(i, par):
                act.wait_ge(xt_psum, i + 1)
                wait(act, gu_psum, i - 1)
                nc.scalar.copy(xTg[:, par].rearrange("p j c t -> p (j c t)"), ps[:, B_XT, :]).then_inc(xt_ready, 1)

            def silu(i, par):
                act.wait_ge(gu_psum, i + 1)
                wait(act, h_ready, i - 1)
                nc.scalar.activation(sg[:, par], ps[:, B_G + 2 * par:B_G + 2 * par + 2, 0:D], ACT.Silu).then_inc(sg_ready, 1)

            def evac_y(o, u):
                i = o * PAIRS + u
                act.wait_ge(y_psum, i + 1)
                wait(act, y_out[u % 2], 32 * (o * (PAIRS // 2) + u // 2))
                nc.scalar.copy(ysb[:, u % 2].rearrange("p j n -> p (j n)"), ps[:, B_Y, :]).then_inc(y_ready, 1)

            def step(o):
                first, last = isinstance(o, int) and o == 0, isinstance(o, int) and o == OUTER - 1
                for u in range(PAIRS):
                    i = o * PAIRS + u
                    if not (last and u == PAIRS - 1):
                        evac_x(i + 1, (u + 1) % 2)
                    silu(i, u % 2)
                    if u > 0:
                        evac_y(o, u - 1)
                    elif not first:
                        evac_y(o - 1, PAIRS - 1)
                    if u % HALF == 1:
                        piece = o * C + u // HALF
                        act.wait_ge(args_ready, piece + 1)
                        nc.scalar.activation(args, args, ACT.Exp).then_inc(exps_ready, 1)

            evac_x(0, 0)
            outer_steps(act, step)
            evac_y(OUTER - 1, PAIRS - 1)
            for n in range(T // 2):
                act.wait_ge(acc_ready, n + 1)
                tt = slice(2 * n, 2 * n + 2)
                nc.scalar.activation(acc[:, tt, :], acc[:, tt, :], ACT.Silu).then_inc(silu_ready, 1)

        @block.tensor
        def _(pe):
            def product(dst, lhsT, rhs):
                for c in range(C):
                    ins = nc.tensor.matmul(dst, lhsT(c), rhs(c), start=(c == 0), stop=(c == C - 1))
                return ins

            pe.wait_ge(consts, 11)
            for b in range(BATCH):
                pe.wait_ge(xn_ready, b + 1)
                for c in range(C):
                    wait(pe, xnt_ready, C * (b - 1) + c + 1)
                    for t in range(TB):
                        ins = nc.tensor.transpose(ps[:, (B_XT, B_Y)[c], t * P:(t + 1) * P],
                                                  x_sb[:, b * TB + t, c * P:(c + 1) * P], ident[:, :])
                    ins.then_inc(xnt_psum, 1)
            pe.wait_ge(small_in, 16 * 6)
            for t in range(T):
                b, s = divmod(t, TB)
                if s == 0:
                    pe.wait_ge(xnt_ready, C * (b + 1))
                ins = product(logits[:, t, :], lambda c: xnT[:, c, b, 1 + s * P:1 + (s + 1) * P], lambda c: wrou[:, c, :])
            ins.then_inc(logits_ready, 1)

            def project(b, between=lambda n: None):
                for w in range(3):
                    pe.wait_ge(mix_ready, 3 * b + w + 1)
                    for c in range(C):
                        n = (b * 3 + w) * C + c
                        wait(pe, proj_out, n - 3)
                        product(ps[:, B_G + n % 4, :], lambda h: wT[w][:, h, c * P:(c + 1) * P],
                                lambda h: mix[w][:, h, :]).then_inc(proj_psum, 1)
                        between(w * C + c)

            def place_rows(t):
                pe.wait_ge(ohA_ready, t + 1)
                pe.wait_ge(ohB_ready, t + 1)
                for s in range(TOPK):
                    ins = nc.tensor.matmul(table, ohB[:, t % 2, s], ohA[:, t % 2, s], start=(t == 0 and s == 0),
                                           stop=(t == T - 1 and s == TOPK - 1))
                ins.then_inc(oh_used, 1)

            project(0)
            pe.wait_ge(sel_ready, 1)
            selr = sel.rearrange("p t e -> p (t e)")
            nc.tensor.matmul(ps[:, B_Y, 0:T * E], upper, selr, start=True, stop=True)
            nc.tensor.matmul(ps[:, B_Y, T * E:2 * T * E], ones, selr, start=True, stop=True).then_inc(count_ready, 1)
            project(1)
            project(2, lambda n: [place_rows(t) for t in range(3 * n, min(3 * n + 3, T))])
            project(3)

            def transpose_x(i, o, u):
                par = u % 2
                pe.wait_ge(xg_in[par], 32 * (o * (PAIRS // 2) + u // 2 + 1))
                wait(pe, xt_ready, i)
                for j in range(2):
                    for c in range(C):
                        ins = nc.tensor.transpose(ps[:, B_XT, (j * C + c) * P:(j * C + c + 1) * P],
                                                  xg[:, par, j, c * P:(c + 1) * P], ident[:, :])
                ins.then_inc(xt_psum, 1)

            def gate_up(par, j, expert):
                return product(ps[:, B_G + 2 * par + j, :], lambda c: xTg[:, par, j, c, :],
                               lambda c: wgu[:, c, bass.ds(expert, 1), :].rearrange("p a n -> p (a n)"))

            def transpose_h(i, par):
                pe.wait_ge(h_ready, i + 1)
                wait(pe, ht_ready, i)
                for j in range(2):
                    for c in range(C):
                        ins = nc.tensor.transpose(ps[:, B_HT, (j * C + c) * P:(j * C + c + 1) * P],
                                                  hid[:, par, j, c * P:(c + 1) * P], ident[:, :])
                ins.then_inc(ht_psum, 1)

            def down(i, par, experts):
                pe.wait_ge(ht_ready, i + 1)
                wait(pe, y_ready, i)
                for j in range(2):
                    ins = product(ps[:, B_Y, j * D:(j + 1) * D], lambda c: hT[:, par, j, c, :],
                                  lambda c: wdn[:, c, bass.ds(experts[j], 1), :].rearrange("p a n -> p (a n)"))
                ins.then_inc(y_psum, 1)

            def experts_of(i):
                return [pe.value_load(tile_expert[0:1, bass.ds(2 * i + j, 1)], min_val=0, max_val=E - 1) for j in range(2)]

            def step(o):
                first, last = isinstance(o, int) and o == 0, isinstance(o, int) and o == OUTER - 1
                for u in range(PAIRS):
                    i = o * PAIRS + u
                    par = u % 2
                    if u < PAIRS - 1:
                        transpose_x(i + 1, o, u + 1)
                    elif not last:
                        transpose_x(i + 1, o + 1, 0)
                    now = experts_of(i)
                    has_before = u > 0 or not first
                    pe.wait_ge(xt_ready, i + 1)
                    wait(pe, h_ready, i - 1)
                    gate_up(par, 0, now[0])
                    if has_before:
                        before = experts_of(i - 1)
                        transpose_h(i - 1, 1 - par)
                    gate_up(par, 1, now[1]).then_inc(gu_psum, 1)
                    if has_before:
                        down(i - 1, 1 - par, before)

            transpose_x(0, 0, 0)
            pe.wait_ge(experts_ready, 1)
            pe.wait_ge(wgu_in, 16 * 4)
            pe.wait_ge(proj_out, BATCH * 3 * C)
            pe.wait_ge(wdn_in, 16 * C)
            outer_steps(pe, step)
            last = experts_of(NP - 1)
            transpose_h(NP - 1, 1)
            down(NP - 1, 1, last)
            pe.wait_ge(wkv_ready, C * BATCH)
            for n in range(T // 2):
                wait(pe, ffn_times_s, n - 3)
                for j in range(2):
                    t = 2 * n + j
                    ins = product(ps[:, B_G + n % 4, j * D:(j + 1) * D], lambda c: rT[:, c, t * P:(t + 1) * P],
                                  lambda c: woT[:, c, :])
                ins.then_inc(s_psum, 1)

        @block.vector
        def _(dve):
            V = nc.vector
            base, done = [0], [0]

            def link(ins):
                done[0] += 1
                ins.then_inc(dve_step, 1)
                dve.wait_ge(dve_step, base[0] + done[0])

            def inner(a, n=E):
                return a.unsqueeze(2).to_broadcast([a.shape[0], a.shape[1], n])

            link(V.memset(xnT[:, :, :, 0:1], 0.0))
            for b in range(BATCH + 1):
                if b < BATCH:
                    dve.wait_ge(x_in_s[b], 16)
                    for t in range(b * TB, (b + 1) * TB):
                        ins = V.bn_stats(stats[:, t, :], x_sb[:, t, :])
                    link(ins)
                    for t in range(b * TB, (b + 1) * TB):
                        ins = V.bn_aggr(mv[:, t, :], stats[:, t, :])
                    ins.then_inc(var_ready, 1)
                if b > 0:
                    dve.wait_ge(rstd_ready, b)
                    if b == 1:
                        dve.wait_ge(var_ready, 1)
                    for t in range((b - 1) * TB, b * TB):
                        ins = V.tensor_scalar(x_sb[:, t, :], x_sb[:, t, :], mv[:, t, 0:1], rstd[:, t:t + 1],
                                              ALU.subtract, ALU.mult)
                    ins.then_inc(xn_ready, 1)
            dve.wait_ge(decay_ready, 1)
            link(V.tensor_scalar(decay[:, :], decay[:, :], -1.0, None, ALU.mult))
            V.memset(eqs[:, 0, 0:1], 0.0).then_inc(zcol, 1)

            def mixes(b):
                dve.wait_ge(diff_ready, b + 1)
                for w in range(3):
                    wait(dve, proj_psum, ((b - 1) * 3 + w + 1) * C)
                    for c in range(C):
                        m = vec[:, (2 + w) * C + c:(2 + w) * C + c + 1]
                        ins = V.scalar_tensor_tensor(out=mix[w][:, c, :], in0=diff[:, c, :], scalar=m,
                                                     in1=xnT[:, c, b, 0:SEQ], op0=ALU.mult, op1=ALU.add)
                    ins.then_inc(mix_ready, 1)

            mixes(0)
            dve.wait_ge(logits_ready, 1)
            link(V.tensor_reduce(rmax, logits, X, ALU.max))
            V.tensor_tensor(z, logits, inner(rmax), ALU.subtract).then_inc(z_ready, 1)
            dve.wait_ge(ez_ready, 1)
            link(V.tensor_reduce(rsum, prob, X, ALU.add))
            link(V.reciprocal(rinv, rsum))
            link(V.tensor_tensor(prob, prob, inner(rinv), ALU.mult))
            for t in range(T):
                ins = V.max(m8[:, t, :], prob[:, t, :])
            link(ins)
            kth = m8[:, :, TOPK - 1]
            dve.wait_ge(consts, 11)
            V.tensor_tensor(gt, prob, inner(kth), ALU.is_gt)
            link(V.tensor_tensor(eq, prob, inner(kth), ALU.is_equal))
            V.tensor_reduce(cgt, gt, X, ALU.add)
            flat = lambda a: a.rearrange("p a b -> p (a b)")
            link(V.tensor_tensor_scan(flat(pre), flat(keep), flat(eq), 0.0, ALU.mult, ALU.add))
            link(V.tensor_tensor(pre, pre, inner(cgt), ALU.add))
            link(V.scalar_tensor_tensor(out=eq, in0=pre, scalar=float(TOPK), in1=eq, op0=ALU.is_le, op1=ALU.mult))
            V.tensor_tensor(sel, gt, eq, ALU.add).then_inc(sel_ready, 1)
            dve.wait_ge(sel_ready, 1)
            link(V.tensor_tensor(wsel, prob, sel, ALU.mult))
            link(V.tensor_reduce(wsum, wsel, X, ALU.add))
            link(V.reciprocal(winv, wsum))
            V.tensor_tensor(coef, wsel, inner(winv), ALU.mult)
            link(V.tensor_tensor_scan(flat(slot), flat(keep), flat(sel), 0.0, ALU.mult, ALU.add))
            link(V.tensor_tensor(slot, slot, sel, ALU.mult))
            mixes(1)
            dve.wait_ge(count_ready, 1)
            link(V.tensor_copy(totT, totals))
            link(V.tensor_tensor_scan(flat(incl), flat(keep), flat(totT), 0.0, ALU.mult, ALU.add))
            V.tensor_tensor(excl, incl, totT, ALU.subtract)
            link(V.tensor_tensor(cmp, inner(incl[:, :, T - 1], T), jrow.unsqueeze(1).to_broadcast([P, E, T]), ALU.is_gt))
            link(V.tensor_reduce(ntile, cmp, X, ALU.add))
            link(V.tensor_tensor_scan(tend, ones16, ntile, 0.0, ALU.mult, ALU.add))
            link(V.tensor_tensor(tstart, tend, ntile, ALU.subtract))
            link(V.scalar_tensor_tensor(out=excl, in0=inner(tstart, T), scalar=float(P), in1=excl, op0=ALU.mult, op1=ALU.add))
            link(V.tensor_tensor(pos, prefix, excl.rearrange("p e t -> p t e"), ALU.add))
            eq4 = eqs.rearrange("p t (s e) -> p t s e", s=TOPK)
            pr4 = prod.rearrange("p t (s e) -> p t s e", s=TOPK)
            by_slot = lambda a: a.unsqueeze(2).to_broadcast([P, T, TOPK, E])
            link(V.tensor_tensor(eq4, by_slot(slot), srow.unsqueeze(1).unsqueeze(3).to_broadcast([P, T, TOPK, E]), ALU.is_equal))
            link(V.tensor_tensor(pr4, eq4, by_slot(pos), ALU.mult))
            link(V.tensor_reduce(pos4, pr4, X, ALU.add))
            link(V.tensor_copy(posi, flat(pos4)))
            V.tensor_scalar(ptilei, posi, 7, None, ALU.logical_shift_right)
            link(V.tensor_scalar(prowi, posi, P - 1, None, ALU.bitwise_and))
            V.tensor_copy(flat(ptile), ptilei)
            V.tensor_copy(flat(prow), prowi).then_inc(digits_ready, 1)
            dve.wait_ge(digits_ready, 1)
            link(V.tensor_tensor(pr4, eq4, by_slot(coef), ALU.mult))
            V.tensor_reduce(coef4[:, :, :], pr4, X, ALU.add)
            mixes(2)
            for t in range(T):
                if t >= 2:
                    dve.wait_ge(oh_used, t - 1)
                for s in range(TOPK):
                    ins = V.tensor_scalar(ohA[:, t % 2, s], iota_row[:, 0:NT], ptile[:, t, s:s + 1], val[:, t, s:s + 1],
                                          ALU.is_equal, ALU.mult)
                ins.then_inc(ohA_ready, 1)
            link(V.tensor_tensor(etmp, tend.unsqueeze(1).to_broadcast([P, NT, E]), inner(iota_row[:, 0:NT]), ALU.is_le))
            link(V.tensor_reduce(esum, etmp, X, ALU.add))
            V.tensor_scalar(tile_expert[:, :], esum[0:1, :], float(E - 1), None, ALU.min).then_inc(experts_ready, 1)
            dve.wait_ge(oh_used, T)
            link(V.tensor_scalar(padt, table, 0.0, padv, ALU.is_equal, ALU.mult))
            link(V.scalar_tensor_tensor(out=dst_idx[:, :], in0=table, scalar=-1.0, in1=padt, op0=ALU.add, op1=ALU.add))
            V.tensor_scalar(tok_idx[:, :], dst_idx[:, :], TOK - 1, None, ALU.bitwise_and).then_inc(index_ready, 1)
            mixes(3)

            def evac_h(i, par):
                dve.wait_ge(ht_psum, i + 1)
                wait(dve, y_psum, i - 1)
                V.tensor_copy(hT[:, par].rearrange("p j c t -> p (j c t)"), ps[:, B_HT, :]).then_inc(ht_ready, 1)

            def hidden(i, par):
                dve.wait_ge(sg_ready, i + 1)
                wait(dve, ht_psum, i - 1)
                V.tensor_tensor(hid[:, par], sg[:, par], ps[:, B_G + 2 * par:B_G + 2 * par + 2, D:2 * D], ALU.mult).then_inc(h_ready, 1)

            def wkv(o, piece_in_step, part):
                c = piece_in_step
                piece = o * C + c
                cols = bass.ds(o * SEQ, SEQ)
                k, v, r = kT[:, c, cols], vT[:, c, cols], rT[:, c, cols]
                w, first = decay[:, c:c + 1], vec[:, C + c:C + c + 1]
                m_old, m_new = mrun[:, 0:SEQ], mrun[:, 1:SEQ + 1]
                e_keep, e_new, o_keep, o_new = (args[:, a, :] for a in range(4))
                if part == 0:
                    V.memset(mrun[:, 0:1], NEG_INF)
                    V.memset(num[:, 0:1], 0.0)
                    V.memset(den[:, 0:1], 0.0)
                    link(V.tensor_tensor_scan(m_new, w.to_broadcast([P, SEQ]), k, NEG_INF, ALU.add, ALU.max))
                    V.scalar_tensor_tensor(out=e_keep, in0=m_old, scalar=w, in1=m_new, op0=ALU.add, op1=ALU.subtract)
                    V.tensor_tensor(e_new, k, m_new, ALU.subtract)
                elif part == 1:
                    link(V.scalar_tensor_tensor(out=ta, in0=k, scalar=first, in1=m_old, op0=ALU.add, op1=ALU.max))
                    V.tensor_tensor(o_keep, m_old, ta, ALU.subtract)
                    V.scalar_tensor_tensor(out=o_new, in0=k, scalar=first, in1=ta, op0=ALU.add,
                                           op1=ALU.subtract).then_inc(args_ready, 1)
                elif part == 2:
                    dve.wait_ge(exps_ready, piece + 1)
                    link(V.tensor_tensor(tb, e_new, v, ALU.mult))
                    V.tensor_tensor_scan(num[:, 1:SEQ + 1], e_keep, tb, 0.0, ALU.mult, ALU.add)
                    link(V.tensor_tensor_scan(den[:, 1:SEQ + 1], e_keep, e_new, 0.0, ALU.mult, ALU.add))
                elif part == 3:
                    V.tensor_tensor(ta, o_new, v, ALU.mult)
                    V.tensor_tensor(tb, o_keep, num[:, 0:SEQ], ALU.mult)
                    link(V.tensor_tensor(o_keep, o_keep, den[:, 0:SEQ], ALU.mult))
                    link(V.tensor_tensor(o_keep, o_keep, o_new, ALU.add))
                else:
                    V.tensor_tensor(ta, ta, tb, ALU.add)
                    link(V.reciprocal(o_keep, o_keep))
                    link(V.tensor_tensor(ta, ta, o_keep, ALU.mult))
                    V.tensor_tensor(r, ta, r, ALU.mult).then_inc(wkv_ready, 1)
                    dve.wait_ge(wkv_ready, piece + 1)

            def step(o):
                first = isinstance(o, int) and o == 0
                for u in range(PAIRS):
                    i = o * PAIRS + u
                    if u > 0 or not first:
                        evac_h(i - 1, (u - 1) % 2)
                    hidden(i, u % 2)
                    wkv(o, u // HALF, u % HALF)

            start = done[0]
            step(0)
            per_step = done[0] - start
            with dve.Fori(1, OUTER - 1) as o:
                done[0] = start
                base[0] = o * per_step
                step(o)
                assert done[0] == start + per_step
            base[0], done[0] = (OUTER - 1) * per_step, start
            step(OUTER - 1)
            evac_h(NP - 1, 1)
            def gated(n):
                tt = slice(2 * n, 2 * n + 2)
                dve.wait_ge(silu_ready, n + 1)
                dve.wait_ge(s_psum, n + 1)
                V.tensor_tensor(acc[:, tt, :], acc[:, tt, :], ps[:, B_G + n % 4, :].rearrange("p (t n) -> p t n", t=2),
                                ALU.mult).then_inc(ffn_times_s, 1)

            for n in range(T // 2):
                dve.wait_ge(y_in[n], 32)
                for s in range(TOPK):
                    for t in (2 * n, 2 * n + 1):
                        cf = coef4[:, t, s:s + 1]
                        if s == 0:
                            ins = V.tensor_scalar(acc[:, t, :], y4[:, t, s, :], cf, None, ALU.mult)
                        else:
                            ins = V.scalar_tensor_tensor(out=acc[:, t, :], in0=y4[:, t, s, :], scalar=cf,
                                                         in1=acc[:, t, :], op0=ALU.mult, op1=ALU.add)
                    if s < TOPK - 1:
                        link(ins)
                ins.then_inc(acc_ready, 1)
                if n > 0:
                    gated(n - 1)
            gated(T // 2 - 1)


def kernel(**inputs):
    import numpy as np
    import concourse.bacc as bacc
    from concourse.bass_utils import run_bass_kernel_spmd

    a = {k.replace("L0_", ""): np.asarray(v) for k, v in inputs.items()}
    vecs = np.stack([a["attn_time_decay"], a["attn_time_first"], a["attn_time_mix_key"].reshape(-1),
                     a["attn_time_mix_value"].reshape(-1), a["attn_time_mix_receptance"].reshape(-1)])
    arrays = {
        "x_in": a["attn_hidden"],
        "vec_in": vecs.reshape(5, C, P).transpose(2, 0, 1).reshape(P, 5 * C),
        "wkT_in": a["attn_Wk"].T, "wvT_in": a["attn_Wv"].T, "wrT_in": a["attn_Wr"].T, "woT_in": a["attn_Wo"].T,
        "wrouT_in": a["ffn_w_router"].T,
        "wg_in": a["ffn_w_gate"], "wu_in": a["ffn_w_up"], "wd_in": a["ffn_w_down"],
    }
    arrays = {k: np.ascontiguousarray(v) for k, v in arrays.items()}
    nc = bacc.Bacc("TRN2", target_bir_lowering=False, num_devices=1)
    args = [nc.dram_tensor(k, v.shape, mybir.dt.from_np(v.dtype), kind="ExternalInput").ap() for k, v in arrays.items()]
    out = nc.dram_tensor("out", arrays["x_in"].shape, mybir.dt.float32, kind="ExternalOutput").ap()
    rwkv_times_moe(nc, *args, out)
    r = run_bass_kernel_spmd(nc, [arrays], core_ids=[0])
    return r.results[0]["out"]
```

```python
import concourse.bass as bass
from concourse import mybir
from contextlib import ExitStack

BATCH, SEQ, D = 4, 512, 256
E, TOPK = 16, 4
P = 128
C = D // P
TOK = BATCH * SEQ
T = TOK // P
TB = SEQ // P
ROWS = TOK * TOPK
OUTER = 4
PAIRS = -(-(ROWS // P + E - 1) // (2 * OUTER))
NP = OUTER * PAIRS
NT = 2 * NP
HALF = PAIRS // C
LN_EPS = 1e-5
NEG_INF = -1e38
assert PAIRS % 2 == 0 and HALF == 5 and C == 2


def rwkv_times_moe(nc, x_in, vec_in, wkT_in, wvT_in, wrT_in, woT_in, wrouT_in, wg_in, wu_in, wd_in, out):
    f32, i32 = mybir.dt.float32, mybir.dt.int32
    ALU = mybir.AluOpType
    ACT = mybir.ActivationFunctionType
    X = mybir.AxisListType.X

    xn_rows = nc.dram_tensor("xn_rows", [TOK, D], f32, kind="Internal").ap()
    y_rows = nc.dram_tensor("y_rows", [ROWS, D], f32, kind="Internal").ap()

    x_v = x_in.rearrange("b (t p) d -> p b t d", p=P)
    out_v = out.rearrange("b (t p) d -> p (b t) d", p=P)
    xn_v = xn_rows.rearrange("(b t p) d -> p b t d", p=P, t=TB)
    y_v = y_rows.rearrange("(s t p) d -> p t s d", p=P, t=T)

    ctx = ExitStack()
    with ctx:
        def sb(name, shape, dt=f32):
            return ctx.enter_context(nc.sbuf_tensor(name, shape, dt))

        def sem(name):
            return ctx.enter_context(nc.semaphore(name))

        wbig = sb("wbig", [P, 3 * C * E * D])
        wgu = wbig[:, 0:2 * C * E * D].rearrange("p (c e n) -> p c e n", c=C, e=E)
        wdn = wbig[:, 2 * C * E * D:].rearrange("p (c e n) -> p c e n", c=C, e=E)
        kT = sb("kT", [P, C, TOK])
        vT = sb("vT", [P, C, TOK])
        rT = sb("rT", [P, C, TOK])
        woT = sb("woT", [P, C, D])
        ident = sb("ident", [P, P])
        vec = sb("vec", [P, 5 * C])
        decay = sb("decay", [P, C])
        tok_idx = sb("tok_idx", [P, NT], i32)
        dst_idx = sb("dst_idx", [P, NT], i32)
        tile_expert = sb("tile_expert", [1, NT], i32)
        coef4 = sb("coef4", [P, T, TOPK])
        xg = sb("xg", [P, 2, 2, D])
        g_idx = sb("g_idx", [P, 2 * PAIRS], i32)
        s_idx = sb("s_idx", [P, 2 * PAIRS], i32)

        XNT = C * BATCH * (SEQ + 1)
        MIXN = C * SEQ
        arena = sb("arena", [P, XNT + 5 * MIXN + 3 * C * D])
        at = [0]

        def carve(n):
            at[0] += n
            return arena[:, at[0] - n:at[0]]

        xnT = carve(XNT).rearrange("p (c b s) -> p c b s", c=C, b=BATCH)
        diff = [carve(MIXN).rearrange("p (c s) -> p c s", c=C) for _ in range(2)]
        mix = [carve(MIXN).rearrange("p (c s) -> p c s", c=C) for _ in range(3)]
        wT = [carve(C * D).rearrange("p (c n) -> p c n", c=C) for _ in range(3)]
        at[0] = 0
        xTg = carve(2 * 2 * D).rearrange("p (b j c t) -> p b j c t", b=2, j=2, c=C)
        sg = carve(2 * 2 * D).rearrange("p (b j n) -> p b j n", b=2, j=2)
        hid = carve(2 * 2 * D).rearrange("p (b j n) -> p b j n", b=2, j=2)
        hT = carve(2 * 2 * D).rearrange("p (b j c t) -> p b j c t", b=2, j=2, c=C)
        ysb = carve(2 * 2 * D).rearrange("p (b j n) -> p b j n", b=2, j=2)
        mrun = carve(SEQ + 1)
        num = carve(SEQ + 1)
        den = carve(SEQ + 1)
        args = carve(4 * SEQ).rearrange("p (a s) -> p a s", a=4)
        ta = carve(SEQ)
        tb = carve(SEQ)
        wrou = sb("wrou", [P, C, E])
        x_sb = rT[:, :, :].rearrange("p c (t n) -> p (c t) n", n=D)

        LATE = 9
        SCRATCH = ((3 * C - 1) * E - LATE) * D
        scr_at = [SCRATCH]

        def scratch(*shape):
            n = 1
            for s in shape:
                n *= s
            v = wbig[:, scr_at[0]:scr_at[0] + n]
            scr_at[0] += n
            assert scr_at[0] <= 3 * C * E * D
            if len(shape) == 1:
                return v
            names = "abc"[:len(shape)]
            return v.rearrange(f"p ({' '.join(names)}) -> p {' '.join(names)}", **dict(zip(names, shape)))

        stats = scratch(T, 6)
        mv = scratch(T, 2)
        veps = scratch(T)
        rstd = scratch(T)
        mhalf = scratch(TB)
        rmax, rsum, rinv, cgt, wsum, winv = (scratch(T) for _ in range(6))
        z, prob, gt, eq, pre, sel, wsel, coef, slot, keep = (scratch(T, E) for _ in range(10))
        pos = z
        totT, incl, excl, cmp = (scratch(E, T) for _ in range(4))
        ntile, tend, tstart, ones16 = (scratch(E) for _ in range(4))
        m8 = scratch(T, 8)
        eqs = xg[:, :, :, :].rearrange("p b j n -> p (b j n)").rearrange("p (t n) -> p t n", t=T)
        prod_etmp = scratch(max(NT, T * TOPK) * E)
        prod = prod_etmp[:, 0:T * TOPK * E].rearrange("p (t n) -> p t n", t=T)
        etmp = prod_etmp[:, 0:NT * E].rearrange("p (t e) -> p t e", e=E)
        pos4, ptile, prow, val = (scratch(T, TOPK) for _ in range(4))
        posi = scratch(T * TOPK).bitcast(i32)
        ptilei = scratch(T * TOPK).bitcast(i32)
        prowi = scratch(T * TOPK).bitcast(i32)
        iota_row = scratch(P)
        jrow = scratch(T)
        srow = scratch(TOPK)
        padv = scratch(1)
        upper = scratch(P)
        ones = scratch(P)
        RING = 4
        ohA = sb("ohA", [P, RING, TOPK, NT])
        ohB = sb("ohB", [P, RING, TOPK, P])
        nbias = scratch(T)
        padt = scratch(NT)
        esum = scratch(NT)

        y4 = wbig[:, 0:T * TOPK * D].rearrange("p (t s n) -> p t s n", t=T, s=TOPK)
        acc = wbig[:, T * TOPK * D:T * (TOPK + 1) * D].rearrange("p (t n) -> p t n", t=T)
        xre = kT[:, :, :].rearrange("p c (t n) -> p (c t) n", n=D)

        ps = ctx.enter_context(nc.psum_tensor("ps", [P, 8, 512], f32))
        B_XT, B_G, B_HT, B_Y, B_R = 0, 1, 5, 6, 7
        logits = ps[:, B_R, 0:T * E].rearrange("p (t e) -> p t e", t=T)
        prefix = ps[:, B_Y, 0:T * E].rearrange("p (t e) -> p t e", t=T)
        totals = ps[:, B_Y, T * E:2 * T * E].rearrange("p (t e) -> p e t", t=T)
        table = ps[:, B_HT, 0:NT]

        x_in_s = [sem(f"x_in{b}") for b in range(BATCH)]
        small_in = sem("small_in")
        wgu_in, wdn_in = sem("wgu_in"), sem("wdn_in")
        xn_stored = sem("xn_stored")
        consts = sem("consts")
        var_ready, rstd_ready, nbias_ready = sem("var_ready"), sem("rstd_ready"), sem("nbias_ready")
        rmul_ready, rmix_ready = sem("rmul_ready"), sem("rmix_ready")
        scaled_ready, half_ready = sem("scaled_ready"), sem("half_ready")
        xn_ready = sem("xn_ready")
        xnt_psum, xnt_ready = sem("xnt_psum"), sem("xnt_ready")
        zcol = sem("zcol")
        diff_ready, mix_ready = sem("diff_ready"), sem("mix_ready")
        decay_ready = sem("decay_ready")
        proj_psum, proj_out = sem("proj_psum"), sem("proj_out")
        logits_ready, z_ready, ez_ready = sem("logits_ready"), sem("z_ready"), sem("ez_ready")
        sel_ready, count_ready = sem("sel_ready"), sem("count_ready")
        digits_ready = sem("digits_ready")
        ohA_ready, ohB_ready, oh_used = sem("ohA_ready"), sem("ohB_ready"), sem("oh_used")
        experts_ready = sem("experts_ready")
        table_ready, index_ready = sem("table_ready"), sem("index_ready")
        pool_turn = sem("pool_turn")
        gi_ready, si_ready = sem("gi_ready"), sem("si_ready")
        xg_in = [sem(f"xg_in{i}") for i in range(2)]
        y_out = [sem(f"y_out{i}") for i in range(2)]
        xt_psum, xt_ready = sem("xt_psum"), sem("xt_ready")
        gu_psum, sg_ready, h_ready = sem("gu_psum"), sem("sg_ready"), sem("h_ready")
        ht_psum, ht_ready = sem("ht_psum"), sem("ht_ready")
        y_psum, y_ready = sem("y_psum"), sem("y_ready")
        args_ready, exps_ready = sem("args_ready"), sem("exps_ready")
        wkv_ready = sem("wkv_ready")
        dve_step, pool_step = sem("dve_step"), sem("pool_step")
        y_in = [sem(f"y_in{i}") for i in range(T // 2)]
        xre_in = sem("xre_in")
        acc_ready, silu_ready, s_psum, ffn_times_s, res_ready = (
            sem("acc_ready"), sem("silu_ready"), sem("s_psum"), sem("ffn_times_s"), sem("res_ready"))
        out_stored = sem("out_stored")

        def wait(eng, s, value):
            if not isinstance(value, int) or value > 0:
                eng.wait_ge(s, value)

        def outer_steps(eng, step):
            step(0)
            with eng.Fori(1, OUTER - 1) as o:
                step(o)
            step(OUTER - 1)

        block = ctx.enter_context(nc.Block())

        @block.sync
        def _(sp):
            for b in range(BATCH):
                sp.dma_start(x_sb[:, b * TB:(b + 1) * TB, :], x_v[:, b]).then_inc(x_in_s[b], 16)
            for dst, src in ((vec[:, :], vec_in), (wrou[:, :, :], wrouT_in.rearrange("(c p) n -> p c n", p=P)),
                             (wT[0], wkT_in.rearrange("(c p) n -> p c n", p=P)),
                             (wT[1], wvT_in.rearrange("(c p) n -> p c n", p=P)),
                             (wT[2], wrT_in.rearrange("(c p) n -> p c n", p=P)),
                             (woT[:, :, :], woT_in.rearrange("(c p) n -> p c n", p=P))):
                sp.dma_start(dst, src).then_inc(small_in, 16)
            for b in range(BATCH):
                sp.wait_ge(xn_ready, b + 1)
                sp.dma_start(xn_v[:, b], x_sb[:, b * TB:(b + 1) * TB, :]).then_inc(xn_stored, 16)
            for half, src in ((0, wg_in), (1, wu_in)):
                for c in range(C):
                    sp.dma_start(wgu[:, c, :, half * D:(half + 1) * D],
                                 src.rearrange("e (c p) n -> c p e n", p=P)[c]).then_inc(wgu_in, 16)
            wd_v = wd_in.rearrange("e (c p) n -> c p e n", p=P)
            for c in range(C - 1):
                last = E - LATE if c == C - 2 else E
                sp.dma_start(wdn[:, c, 0:last], wd_v[c][:, 0:last]).then_inc(wdn_in, 16)
            sp.wait_ge(index_ready, 1)
            sp.dma_start(wdn[:, C - 2, E - LATE:], wd_v[C - 2][:, E - LATE:]).then_inc(wdn_in, 16)
            sp.dma_start(wdn[:, C - 1], wd_v[C - 1]).then_inc(wdn_in, 16)
            sp.wait_ge(wkv_ready, C * BATCH)
            sp.dma_start(xre, x_in.rearrange("b (t p) d -> p (b t) d", p=P)).then_inc(xre_in, 16)
            sp.wait_ge(y_psum, NP)
            for i in range(2):
                sp.wait_ge(y_out[i], 32 * (NP // 2))
            for t in range(T):
                sp.dma_start(y4[:, t], y_v[:, t]).then_inc(y_in[t // 2], 16)
            for n in range(T // 2):
                sp.wait_ge(res_ready, n + 1)
                sp.dma_start(out_v[:, 2 * n:2 * n + 2, :], acc[:, 2 * n:2 * n + 2, :]).then_inc(out_stored, 16)
            sp.wait_ge(out_stored, 16 * (T // 2))

        @block.gpsimd
        def _(pool):
            done = [0]

            def link(ins):
                done[0] += 1
                ins.then_inc(pool_step, 1)
                pool.wait_ge(pool_step, done[0])

            link(pool.memset(ident[:, :], 0.0))
            pool.affine_select(out=ident[:, :], in_=ident[:, :], compare_op=ALU.not_equal, fill=1.0,
                               base=0, pattern=[[-1, P]], channel_multiplier=1).then_inc(consts, 1)
            pool.memset(mhalf, -0.5).then_inc(consts, 1)
            link(pool.memset(keep, 1.0))
            pool.memset(keep[:, :, 0:1], 0.0).then_inc(consts, 1)
            pool.memset(ones, 1.0).then_inc(consts, 1)
            pool.memset(ones16, 1.0).then_inc(consts, 1)
            link(pool.memset(upper, 1.0))
            pool.affine_select(out=upper, in_=upper, compare_op=ALU.is_gt, fill=0.0,
                               base=0, pattern=[[1, P]], channel_multiplier=-1).then_inc(consts, 1)
            for dst, pattern, base, chan in ((iota_row, [[1, P]], 0, 0), (jrow, [[P, T]], 0, 0),
                                             (srow, [[1, TOPK]], 1, 0), (padv, [[1, 1]], ROWS + 1, 1),
                                             (val, [[P, T], [TOK, TOPK]], 1, 1)):
                pool.iota(dst, pattern, base=base, channel_multiplier=chan,
                          allow_small_or_imprecise_dtypes=True).then_inc(consts, 1)
            N_CONSTS = 11
            pool.wait_ge(consts, N_CONSTS)
            for b in range(BATCH):
                t = slice(b * TB, (b + 1) * TB)
                pool.wait_ge(var_ready, b + 1)
                link(pool.tensor_scalar(veps[:, t], mv[:, t, 1], LN_EPS, None, ALU.add))
                pool.tensor_tensor(rstd[:, t], veps[:, t], mhalf, ALU.pow).then_inc(rstd_ready, 1)
            def token_diff(b):
                pool.wait_ge(xnt_ready, C * (b + 1))
                if b == 0:
                    pool.wait_ge(zcol, 1)
                if b >= 2:
                    pool.wait_ge(mix_ready, 2 * (b - 1))
                    pool.wait_ge(rmul_ready, b - 1)
                pool.tensor_tensor(diff[b % 2], xnT[:, :, b, 1:SEQ + 1], xnT[:, :, b, 0:SEQ], ALU.subtract).then_inc(diff_ready, 1)

            def receptance_mix(b):
                pool.wait_ge(rmul_ready, b + 1)
                pool.tensor_tensor(mix[2], mix[2], xnT[:, :, b, 0:SEQ], ALU.add).then_inc(rmix_ready, 1)

            token_diff(0)
            token_diff(1)
            receptance_mix(0)
            token_diff(2)
            receptance_mix(1)
            token_diff(3)
            pool.wait_ge(digits_ready, 1)
            for t in range(T):
                if t == 2:
                    receptance_mix(2)
                if t == 10:
                    receptance_mix(3)
                if t >= RING:
                    pool.wait_ge(oh_used, t - RING + 1)
                for s in range(TOPK // 2, TOPK):
                    ins = pool.tensor_scalar(ohB[:, t % RING, s], iota_row, prow[:, t, s:s + 1], None, ALU.is_equal)
                ins.then_inc(ohB_ready, 1)

            LAG = 4
            pool.wait_ge(index_ready, 1)
            pool.wait_ge(xn_stored, 16 * BATCH)

            def wait_alone(s, value):
                wait(pool, s, value)
                if not isinstance(value, int):
                    pool.sem_inc(pool_turn, 1)

            def indices(o, dst, src, landed, ready):
                for par in range(2):
                    wait_alone(landed[par], 16 * PAIRS * o)
                pool.tensor_copy(dst[:, :], src[:, bass.ds(2 * PAIRS * o, 2 * PAIRS)]).then_inc(ready, 1)
                wait_alone(ready, o + 1)

            def gather(o, u):
                par = u % 2
                wait_alone(xt_psum, o * PAIRS + u - 1)
                for j in range(2):
                    n = 2 * u + j
                    pool.indirect_dma_start(out=xg[:, par, j, :], out_offset=None, in_=xn_rows,
                                            in_offset=bass.IndirectOffsetOnAxis(ap=g_idx[:, n:n + 1], axis=0)
                                            ).then_inc(xg_in[par], 16)

            def scatter(o, u):
                par = u % 2
                wait_alone(y_ready, o * PAIRS + u + 1)
                for j in range(2):
                    n = 2 * u + j
                    pool.indirect_dma_start(out=y_rows, in_=ysb[:, par, j, :], in_offset=None,
                                            out_offset=bass.IndirectOffsetOnAxis(ap=s_idx[:, n:n + 1], axis=0),
                                            bounds_check=last_row, oob_is_err=False).then_inc(y_out[par], 16)

            last_row = pool.to_reg(ROWS - 1)

            def step(o):
                indices(o, g_idx, tok_idx, xg_in, gi_ready)
                for u in range(PAIRS):
                    gather(o, u)
                    if u == LAG:
                        indices(o, s_idx, dst_idx, y_out, si_ready)
                    if u >= LAG:
                        scatter(o, u - LAG)
                    elif not isinstance(o, int) or o > 0:
                        scatter(o - 1, u - LAG + PAIRS)

            outer_steps(pool, step)
            for u in range(PAIRS - LAG, PAIRS):
                scatter(OUTER - 1, u)
            def first_slots(n):
                tt = slice(2 * n, 2 * n + 2)
                pool.wait_ge(scaled_ready, n + 1)
                pool.tensor_tensor(acc[:, tt, :], y4[:, tt, 0, :], y4[:, tt, 1, :], ALU.add).then_inc(half_ready, 1)

            def residual(n):
                tt = slice(2 * n, 2 * n + 2)
                pool.wait_ge(ffn_times_s, n + 1)
                pool.tensor_tensor(acc[:, tt, :], acc[:, tt, :], xre[:, tt, :], ALU.add).then_inc(res_ready, 1)

            pool.wait_ge(xre_in, 16)
            for n in range(T // 2 + 2):
                if n < T // 2:
                    first_slots(n)
                if n >= 2:
                    residual(n - 2)

        @block.scalar
        def _(act):
            def normalise(b):
                act.wait_ge(nbias_ready, b + 1)
                for t in range(b * TB, (b + 1) * TB):
                    ins = nc.scalar.activation(x_sb[:, t, :], x_sb[:, t, :], ACT.Identity,
                                               bias=nbias[:, t:t + 1], scale=rstd[:, t:t + 1])
                ins.then_inc(xn_ready, 1)

            def evac_xnt(b):
                for c in range(C):
                    act.wait_ge(xnt_psum, C * b + c + 1)
                    nc.scalar.copy(xnT[:, c, b, 1:SEQ + 1], ps[:, (B_XT, B_Y)[c], :]).then_inc(xnt_ready, 1)

            def scale_diff(b):
                act.wait_ge(diff_ready, b + 1)
                if b == 0:
                    act.wait_ge(small_in, 16 * 6)
                wait(act, proj_psum, b * 3 * C)
                for c in range(C):
                    ins = nc.scalar.activation(mix[2][:, c, :], diff[b % 2][:, c, :], ACT.Copy,
                                               scale=vec[:, 4 * C + c:4 * C + c + 1])
                ins.then_inc(rmul_ready, 1)

            for b in range(BATCH):
                normalise(b)
                if b > 0:
                    evac_xnt(b - 1)
            evac_xnt(BATCH - 1)
            scale_diff(0)
            nc.scalar.activation(decay[:, :], vec[:, 0:C], ACT.Exp).then_inc(decay_ready, 1)
            act.wait_ge(z_ready, 1)
            nc.scalar.activation(prob, z, ACT.Exp).then_inc(ez_ready, 1)
            for b in range(BATCH):
                for w in range(3):
                    for c in range(C):
                        n = (b * 3 + w) * C + c
                        act.wait_ge(proj_psum, n + 1)
                        dst = (kT, vT, rT)[w][:, c, b * SEQ:(b + 1) * SEQ]
                        src = ps[:, B_G + n % 4, :]
                        if w == 2 and n < 3 * C:
                            act.wait_ge(xn_stored, 16 * BATCH)
                        if w == 2:
                            nc.scalar.activation(dst, src, ACT.Sigmoid).then_inc(proj_out, 1)
                        else:
                            nc.scalar.copy(dst, src).then_inc(proj_out, 1)
                if b + 1 < BATCH:
                    scale_diff(b + 1)

            def evac_x(i, par):
                act.wait_ge(xt_psum, i + 1)
                wait(act, gu_psum, i - 1)
                nc.scalar.copy(xTg[:, par].rearrange("p j c t -> p (j c t)"), ps[:, B_XT, :]).then_inc(xt_ready, 1)

            def silu(i, par):
                act.wait_ge(gu_psum, i + 1)
                wait(act, h_ready, i - 1)
                nc.scalar.activation(sg[:, par], ps[:, B_G + 2 * par:B_G + 2 * par + 2, 0:D], ACT.Silu).then_inc(sg_ready, 1)

            def evac_y(o, u):
                i = o * PAIRS + u
                act.wait_ge(y_psum, i + 1)
                wait(act, y_out[u % 2], 32 * (o * (PAIRS // 2) + u // 2))
                nc.scalar.copy(ysb[:, u % 2].rearrange("p j n -> p (j n)"), ps[:, B_Y, :]).then_inc(y_ready, 1)

            def step(o):
                first, last = isinstance(o, int) and o == 0, isinstance(o, int) and o == OUTER - 1
                for u in range(PAIRS):
                    i = o * PAIRS + u
                    if not (last and u == PAIRS - 1):
                        evac_x(i + 1, (u + 1) % 2)
                    silu(i, u % 2)
                    if u % HALF == 1:
                        piece = o * C + u // HALF
                        act.wait_ge(args_ready, piece + 1)
                        nc.scalar.activation(args, args, ACT.Exp).then_inc(exps_ready, 1)
                    if u > 0:
                        evac_y(o, u - 1)
                    elif not first:
                        evac_y(o - 1, PAIRS - 1)

            evac_x(0, 0)
            outer_steps(act, step)
            evac_y(OUTER - 1, PAIRS - 1)
            def scaled(n):
                act.wait_ge(y_in[n], 32)
                for t in (2 * n, 2 * n + 1):
                    for k in range(2):
                        ins = nc.scalar.activation(y4[:, t, k, :], y4[:, t, k, :], ACT.Copy, scale=coef4[:, t, k:k + 1])
                ins.then_inc(scaled_ready, 1)

            def silu_sum(n):
                act.wait_ge(acc_ready, n + 1)
                tt = slice(2 * n, 2 * n + 2)
                nc.scalar.activation(acc[:, tt, :], acc[:, tt, :], ACT.Silu).then_inc(silu_ready, 1)

            for n in range(T // 2 + 1):
                if n < T // 2:
                    scaled(n)
                if n > 0:
                    silu_sum(n - 1)

        @block.tensor
        def _(pe):
            def product(dst, lhsT, rhs):
                for c in range(C):
                    ins = nc.tensor.matmul(dst, lhsT(c), rhs(c), start=(c == 0), stop=(c == C - 1))
                return ins

            def transpose_xn(b):
                pe.wait_ge(xn_ready, b + 1)
                for c in range(C):
                    wait(pe, xnt_ready, C * (b - 1) + c + 1)
                    for t in range(TB):
                        ins = nc.tensor.transpose(ps[:, (B_XT, B_Y)[c], t * P:(t + 1) * P],
                                                  x_sb[:, b * TB + t, c * P:(c + 1) * P], ident[:, :])
                    ins.then_inc(xnt_psum, 1)

            def route(b):
                pe.wait_ge(xnt_ready, C * (b + 1))
                for s in range(TB):
                    ins = product(logits[:, b * TB + s, :], lambda c: xnT[:, c, b, 1 + s * P:1 + (s + 1) * P],
                                  lambda c: wrou[:, c, :])
                ins.then_inc(logits_ready, 1)

            pe.wait_ge(consts, 11)
            transpose_xn(0)
            pe.wait_ge(small_in, 16 * 6)
            for b in range(1, BATCH):
                transpose_xn(b)
                route(b - 1)
            route(BATCH - 1)

            def project(b, between=lambda n: None):
                for w in range(3):
                    if w < 2:
                        pe.wait_ge(mix_ready, 2 * b + w + 1)
                    else:
                        pe.wait_ge(rmix_ready, b + 1)
                    for c in range(C):
                        n = (b * 3 + w) * C + c
                        wait(pe, proj_out, n - 3)
                        product(ps[:, B_G + n % 4, :], lambda h: wT[w][:, h, c * P:(c + 1) * P],
                                lambda h: mix[w][:, h, :]).then_inc(proj_psum, 1)
                        between(w * C + c)

            def count_rows(n):
                if n == 3:
                    pe.wait_ge(sel_ready, 1)
                    selr = sel.rearrange("p t e -> p (t e)")
                    nc.tensor.matmul(ps[:, B_Y, 0:T * E], upper, selr, start=True, stop=True)
                    nc.tensor.matmul(ps[:, B_Y, T * E:2 * T * E], ones, selr, start=True, stop=True).then_inc(count_ready, 1)

            placed = [0]

            def place_rows(tiles):
                for t in range(placed[0], placed[0] + tiles):
                    pe.wait_ge(ohA_ready, t + 1)
                    pe.wait_ge(ohB_ready, t + 1)
                    for s in range(TOPK):
                        ins = nc.tensor.matmul(table, ohB[:, t % RING, s], ohA[:, t % RING, s], start=(t == 0 and s == 0),
                                               stop=(t == T - 1 and s == TOPK - 1))
                    ins.then_inc(oh_used, 1)
                placed[0] += tiles

            project(0, count_rows)
            project(1)
            project(2, lambda n: place_rows((0, 1, 1, 2, 2, 2)[n]))
            project(3, lambda n: place_rows((2, 2, 2, 2, 0, 0)[n]))
            assert placed[0] == T

            def transpose_x(i, o, u):
                par = u % 2
                pe.wait_ge(xg_in[par], 32 * (o * (PAIRS // 2) + u // 2 + 1))
                wait(pe, xt_ready, i)
                for j in range(2):
                    for c in range(C):
                        ins = nc.tensor.transpose(ps[:, B_XT, (j * C + c) * P:(j * C + c + 1) * P],
                                                  xg[:, par, j, c * P:(c + 1) * P], ident[:, :])
                ins.then_inc(xt_psum, 1)

            def gate_up(par, j, expert):
                return product(ps[:, B_G + 2 * par + j, :], lambda c: xTg[:, par, j, c, :],
                               lambda c: wgu[:, c, bass.ds(expert, 1), :].rearrange("p a n -> p (a n)"))

            def transpose_h(i, par):
                pe.wait_ge(h_ready, i + 1)
                wait(pe, ht_ready, i)
                for j in range(2):
                    for c in range(C):
                        ins = nc.tensor.transpose(ps[:, B_HT, (j * C + c) * P:(j * C + c + 1) * P],
                                                  hid[:, par, j, c * P:(c + 1) * P], ident[:, :])
                ins.then_inc(ht_psum, 1)

            def down(i, par, experts):
                pe.wait_ge(ht_ready, i + 1)
                wait(pe, y_ready, i)
                for j in range(2):
                    ins = product(ps[:, B_Y, j * D:(j + 1) * D], lambda c: hT[:, par, j, c, :],
                                  lambda c: wdn[:, c, bass.ds(experts[j], 1), :].rearrange("p a n -> p (a n)"))
                ins.then_inc(y_psum, 1)

            def experts_of(i):
                return [pe.value_load(tile_expert[0:1, bass.ds(2 * i + j, 1)], min_val=0, max_val=E - 1) for j in range(2)]

            def step(o):
                first, last = isinstance(o, int) and o == 0, isinstance(o, int) and o == OUTER - 1
                for u in range(PAIRS):
                    i = o * PAIRS + u
                    par = u % 2
                    if u < PAIRS - 1:
                        transpose_x(i + 1, o, u + 1)
                    elif not last:
                        transpose_x(i + 1, o + 1, 0)
                    now = experts_of(i)
                    has_before = u > 0 or not first
                    pe.wait_ge(xt_ready, i + 1)
                    wait(pe, h_ready, i - 1)
                    gate_up(par, 0, now[0])
                    if has_before:
                        before = experts_of(i - 1)
                        transpose_h(i - 1, 1 - par)
                    gate_up(par, 1, now[1]).then_inc(gu_psum, 1)
                    if has_before:
                        down(i - 1, 1 - par, before)

            transpose_x(0, 0, 0)
            pe.wait_ge(experts_ready, 1)
            pe.wait_ge(wgu_in, 16 * 4)
            pe.wait_ge(proj_out, BATCH * 3 * C)
            pe.wait_ge(wdn_in, 16 * (C + 1))
            outer_steps(pe, step)
            last = experts_of(NP - 1)
            transpose_h(NP - 1, 1)
            down(NP - 1, 1, last)
            pe.wait_ge(wkv_ready, C * BATCH)
            for n in range(T // 2):
                wait(pe, ffn_times_s, n - 3)
                for j in range(2):
                    t = 2 * n + j
                    ins = product(ps[:, B_G + n % 4, j * D:(j + 1) * D], lambda c: rT[:, c, t * P:(t + 1) * P],
                                  lambda c: woT[:, c, :])
                ins.then_inc(s_psum, 1)

        @block.vector
        def _(dve):
            V = nc.vector
            base, done = [0], [0]

            def link(ins):
                done[0] += 1
                ins.then_inc(dve_step, 1)
                dve.wait_ge(dve_step, base[0] + done[0])

            def inner(a, n=E):
                return a.unsqueeze(2).to_broadcast([a.shape[0], a.shape[1], n])

            V.memset(xnT[:, :, :, 0:1], 0.0).then_inc(zcol, 1)
            for b in range(BATCH + 1):
                if b < BATCH:
                    dve.wait_ge(x_in_s[b], 16)
                    for t in range(b * TB, (b + 1) * TB):
                        ins = V.bn_stats(stats[:, t, :], x_sb[:, t, :])
                    link(ins)
                    for t in range(b * TB, (b + 1) * TB):
                        ins = V.bn_aggr(mv[:, t, :], stats[:, t, :])
                    ins.then_inc(var_ready, 1)
                if b > 0:
                    t = slice((b - 1) * TB, b * TB)
                    dve.wait_ge(rstd_ready, b)
                    dve.wait_ge(var_ready, b)
                    V.scalar_tensor_tensor(out=nbias[:, t], in0=mv[:, t, 0], scalar=-1.0, in1=rstd[:, t],
                                           op0=ALU.mult, op1=ALU.mult).then_inc(nbias_ready, 1)

            def mixes(b):
                dve.wait_ge(diff_ready, b + 1)
                if b == 0:
                    dve.wait_ge(small_in, 16 * 6)
                for w in range(2):
                    wait(dve, proj_psum, ((b - 1) * 3 + w + 1) * C)
                    for c in range(C):
                        m = vec[:, (2 + w) * C + c:(2 + w) * C + c + 1]
                        ins = V.scalar_tensor_tensor(out=mix[w][:, c, :], in0=diff[b % 2][:, c, :], scalar=m,
                                                     in1=xnT[:, c, b, 0:SEQ], op0=ALU.mult, op1=ALU.add)
                    ins.then_inc(mix_ready, 1)

            mixes(0)
            dve.wait_ge(logits_ready, BATCH)
            link(V.tensor_reduce(rmax, logits, X, ALU.max))
            V.tensor_tensor(z, logits, inner(rmax), ALU.subtract).then_inc(z_ready, 1)
            dve.wait_ge(ez_ready, 1)
            link(V.tensor_reduce(rsum, prob, X, ALU.add))
            link(V.reciprocal(rinv, rsum))
            link(V.tensor_tensor(prob, prob, inner(rinv), ALU.mult))
            for t in range(T):
                ins = V.max(m8[:, t, :], prob[:, t, :])
            link(ins)
            kth = m8[:, :, TOPK - 1]
            dve.wait_ge(consts, 11)
            V.tensor_tensor(gt, prob, inner(kth), ALU.is_gt)
            link(V.tensor_tensor(eq, prob, inner(kth), ALU.is_equal))
            V.tensor_reduce(cgt, gt, X, ALU.add)
            flat = lambda a: a.rearrange("p a b -> p (a b)")
            link(V.tensor_tensor_scan(flat(pre), flat(keep), flat(eq), 0.0, ALU.mult, ALU.add))
            link(V.tensor_tensor(pre, pre, inner(cgt), ALU.add))
            link(V.scalar_tensor_tensor(out=eq, in0=pre, scalar=float(TOPK), in1=eq, op0=ALU.is_le, op1=ALU.mult))
            V.tensor_tensor(sel, gt, eq, ALU.add).then_inc(sel_ready, 1)
            dve.wait_ge(sel_ready, 1)
            link(V.tensor_tensor(wsel, prob, sel, ALU.mult))
            link(V.tensor_reduce(wsum, wsel, X, ALU.add))
            link(V.reciprocal(winv, wsum))
            V.tensor_tensor(coef, wsel, inner(winv), ALU.mult)
            link(V.tensor_tensor_scan(flat(slot), flat(keep), flat(sel), 0.0, ALU.mult, ALU.add))
            link(V.tensor_tensor(slot, slot, sel, ALU.mult))
            dve.wait_ge(decay_ready, 1)
            link(V.tensor_scalar(decay[:, :], decay[:, :], -1.0, None, ALU.mult))
            mixes(1)
            dve.wait_ge(count_ready, 1)
            link(V.tensor_copy(totT, totals))
            link(V.tensor_tensor_scan(flat(incl), flat(keep), flat(totT), 0.0, ALU.mult, ALU.add))
            V.tensor_tensor(excl, incl, totT, ALU.subtract)
            link(V.tensor_tensor(cmp, inner(incl[:, :, T - 1], T), jrow.unsqueeze(1).to_broadcast([P, E, T]), ALU.is_gt))
            link(V.tensor_reduce(ntile, cmp, X, ALU.add))
            link(V.tensor_tensor_scan(tend, ones16, ntile, 0.0, ALU.mult, ALU.add))
            link(V.tensor_tensor(tstart, tend, ntile, ALU.subtract))
            link(V.scalar_tensor_tensor(out=excl, in0=inner(tstart, T), scalar=float(P), in1=excl, op0=ALU.mult, op1=ALU.add))
            link(V.tensor_tensor(pos, prefix, excl.rearrange("p e t -> p t e"), ALU.add))
            eq4 = eqs.rearrange("p t (s e) -> p t s e", s=TOPK)
            pr4 = prod.rearrange("p t (s e) -> p t s e", s=TOPK)
            by_slot = lambda a: a.unsqueeze(2).to_broadcast([P, T, TOPK, E])
            link(V.tensor_tensor(eq4, by_slot(slot), srow.unsqueeze(1).unsqueeze(3).to_broadcast([P, T, TOPK, E]), ALU.is_equal))
            link(V.tensor_tensor(pr4, eq4, by_slot(pos), ALU.mult))
            link(V.tensor_reduce(pos4, pr4, X, ALU.add))
            link(V.tensor_copy(posi, flat(pos4)))
            V.tensor_scalar(ptilei, posi, 7, None, ALU.logical_shift_right)
            link(V.tensor_scalar(prowi, posi, P - 1, None, ALU.bitwise_and))
            V.tensor_copy(flat(ptile), ptilei)
            V.tensor_copy(flat(prow), prowi).then_inc(digits_ready, 1)
            mixes(2)
            dve.wait_ge(digits_ready, 1)
            for t in range(T):
                if t == T // 2:
                    mixes(3)
                if t >= RING:
                    dve.wait_ge(oh_used, t - RING + 1)
                for s in range(TOPK // 2):
                    V.tensor_scalar(ohB[:, t % RING, s], iota_row, prow[:, t, s:s + 1], None, ALU.is_equal)
                for s in range(TOPK):
                    ins = V.tensor_scalar(ohA[:, t % RING, s], iota_row[:, 0:NT], ptile[:, t, s:s + 1], val[:, t, s:s + 1],
                                          ALU.is_equal, ALU.mult)
                ins.then_inc(ohA_ready, 1)
            link(V.tensor_tensor(pr4, eq4, by_slot(coef), ALU.mult))
            link(V.tensor_reduce(coef4[:, :, :], pr4, X, ALU.add))
            link(V.tensor_tensor(etmp, tend.unsqueeze(1).to_broadcast([P, NT, E]), inner(iota_row[:, 0:NT]), ALU.is_le))
            link(V.tensor_reduce(esum, etmp, X, ALU.add))
            V.tensor_scalar(tile_expert[:, :], esum[0:1, :], float(E - 1), None, ALU.min).then_inc(experts_ready, 1)
            dve.wait_ge(oh_used, T)
            link(V.tensor_scalar(padt, table, 0.0, padv, ALU.is_equal, ALU.mult))
            link(V.scalar_tensor_tensor(out=dst_idx[:, :], in0=table, scalar=-1.0, in1=padt, op0=ALU.add, op1=ALU.add))
            V.tensor_scalar(tok_idx[:, :], dst_idx[:, :], TOK - 1, None, ALU.bitwise_and).then_inc(index_ready, 1)

            def evac_h(i, par):
                dve.wait_ge(ht_psum, i + 1)
                wait(dve, y_psum, i - 1)
                V.tensor_copy(hT[:, par].rearrange("p j c t -> p (j c t)"), ps[:, B_HT, :]).then_inc(ht_ready, 1)

            def hidden(i, par):
                dve.wait_ge(sg_ready, i + 1)
                wait(dve, ht_psum, i - 1)
                V.tensor_tensor(hid[:, par], sg[:, par], ps[:, B_G + 2 * par:B_G + 2 * par + 2, D:2 * D], ALU.mult).then_inc(h_ready, 1)

            def wkv(o, c, part):
                piece = o * C + c
                cols = bass.ds(o * SEQ, SEQ)
                k, v, r = kT[:, c, cols], vT[:, c, cols], rT[:, c, cols]
                w, first = decay[:, c:c + 1], vec[:, C + c:C + c + 1]
                m_old, m_new = mrun[:, 0:SEQ], mrun[:, 1:SEQ + 1]
                e_keep, e_new, o_keep, o_new = (args[:, a, :] for a in range(4))
                H = SEQ // 2
                if part == 0:
                    V.memset(mrun[:, 0:1], NEG_INF)
                    V.memset(num[:, 0:1], 0.0)
                    V.memset(den[:, 0:1], 0.0)
                    link(V.tensor_tensor_scan(m_new, w.to_broadcast([P, SEQ]), k, NEG_INF, ALU.add, ALU.max))
                elif part == 1:
                    V.scalar_tensor_tensor(out=e_keep, in0=m_old, scalar=w, in1=m_new, op0=ALU.add, op1=ALU.subtract)
                    V.tensor_tensor(e_new, k, m_new, ALU.subtract)
                    link(V.scalar_tensor_tensor(out=ta, in0=k, scalar=first, in1=m_old, op0=ALU.add, op1=ALU.max))
                elif part == 2:
                    V.tensor_tensor(o_keep, m_old, ta, ALU.subtract)
                    V.scalar_tensor_tensor(out=o_new, in0=k, scalar=first, in1=ta, op0=ALU.add,
                                           op1=ALU.subtract).then_inc(args_ready, 1)
                elif part == 4:
                    dve.wait_ge(exps_ready, piece + 1)
                    link(V.tensor_tensor(tb, e_new, v, ALU.mult))
                    link(V.tensor_tensor_scan(num[:, 1:SEQ + 1], e_keep, tb, 0.0, ALU.mult, ALU.add))
                elif part == 5:
                    V.tensor_tensor_scan(den[:, 1:SEQ + 1], e_keep, e_new, 0.0, ALU.mult, ALU.add)
                    V.tensor_tensor(ta, o_new, v, ALU.mult)
                    link(V.tensor_tensor(tb, o_keep, num[:, 0:SEQ], ALU.mult))
                elif part == 6:
                    V.tensor_tensor(ta, ta, tb, ALU.add)
                    link(V.tensor_tensor(o_keep, o_keep, den[:, 0:SEQ], ALU.mult))
                elif part == 7:
                    link(V.tensor_tensor(o_keep, o_keep, o_new, ALU.add))
                    V.reciprocal(o_keep[:, 0:H], o_keep[:, 0:H])
                elif part == 8:
                    link(V.reciprocal(o_keep[:, H:SEQ], o_keep[:, H:SEQ]))
                elif part == 9:
                    link(V.tensor_tensor(ta, ta, o_keep, ALU.mult))
                    V.tensor_tensor(r, ta, r, ALU.mult).then_inc(wkv_ready, 1)
                    dve.wait_ge(wkv_ready, piece + 1)

            def step(o):
                first = isinstance(o, int) and o == 0
                for u in range(PAIRS):
                    i = o * PAIRS + u
                    if u > 0 or not first:
                        evac_h(i - 1, (u - 1) % 2)
                    wkv(o, u // HALF, 2 * (u % HALF))
                    hidden(i, u % 2)
                    wkv(o, u // HALF, 2 * (u % HALF) + 1)

            start = done[0]
            step(0)
            per_step = done[0] - start
            with dve.Fori(1, OUTER - 1) as o:
                done[0] = start
                base[0] = o * per_step
                step(o)
                assert done[0] == start + per_step
            base[0], done[0] = (OUTER - 1) * per_step, start
            step(OUTER - 1)
            evac_h(NP - 1, 1)
            def gated(n):
                tt = slice(2 * n, 2 * n + 2)
                dve.wait_ge(silu_ready, n + 1)
                dve.wait_ge(s_psum, n + 1)
                V.tensor_tensor(acc[:, tt, :], acc[:, tt, :], ps[:, B_G + n % 4, :].rearrange("p (t n) -> p t n", t=2),
                                ALU.mult).then_inc(ffn_times_s, 1)

            for n in range(T // 2):
                dve.wait_ge(half_ready, n + 1)
                for s in (2, 3):
                    for t in (2 * n, 2 * n + 1):
                        ins = V.scalar_tensor_tensor(out=acc[:, t, :], in0=y4[:, t, s, :], scalar=coef4[:, t, s:s + 1],
                                                     in1=acc[:, t, :], op0=ALU.mult, op1=ALU.add)
                    if s == 2:
                        link(ins)
                ins.then_inc(acc_ready, 1)
                if n > 0:
                    gated(n - 1)
            gated(T // 2 - 1)


def kernel(**inputs):
    import numpy as np
    import concourse.bacc as bacc
    from concourse.bass_utils import run_bass_kernel_spmd

    a = {k.replace("L0_", ""): np.asarray(v) for k, v in inputs.items()}
    vecs = np.stack([a["attn_time_decay"], a["attn_time_first"], a["attn_time_mix_key"].reshape(-1),
                     a["attn_time_mix_value"].reshape(-1), a["attn_time_mix_receptance"].reshape(-1)])
    arrays = {
        "x_in": a["attn_hidden"],
        "vec_in": vecs.reshape(5, C, P).transpose(2, 0, 1).reshape(P, 5 * C),
        "wkT_in": a["attn_Wk"].T, "wvT_in": a["attn_Wv"].T, "wrT_in": a["attn_Wr"].T, "woT_in": a["attn_Wo"].T,
        "wrouT_in": a["ffn_w_router"].T,
        "wg_in": a["ffn_w_gate"], "wu_in": a["ffn_w_up"], "wd_in": a["ffn_w_down"],
    }
    arrays = {k: np.ascontiguousarray(v) for k, v in arrays.items()}
    nc = bacc.Bacc("TRN2", target_bir_lowering=False, num_devices=1)
    args = [nc.dram_tensor(k, v.shape, mybir.dt.from_np(v.dtype), kind="ExternalInput").ap() for k, v in arrays.items()]
    out = nc.dram_tensor("out", arrays["x_in"].shape, mybir.dt.float32, kind="ExternalOutput").ap()
    rwkv_times_moe(nc, *args, out)
    r = run_bass_kernel_spmd(nc, [arrays], core_ids=[0])
    return r.results[0]["out"]
```

```python
import concourse.bass as bass
from concourse import mybir
from contextlib import ExitStack

BATCH, SEQ, D = 4, 512, 256
E, TOPK = 16, 4
P = 128
C = D // P
TOK = BATCH * SEQ
T = TOK // P
TB = SEQ // P
ROWS = TOK * TOPK
OUTER = 4
NEED = ROWS // P // 2
PAIRS = NEED // OUTER
BLOCKS = -(-(E - 1) // 4)
NP = NEED + 2 * BLOCKS
NT = 2 * NP
HALF = PAIRS // C
LN_EPS = 1e-5
NEG_INF = -1e38
assert OUTER * PAIRS == NEED and PAIRS % 2 == 0 and HALF == 4 and C == 2 and BATCH == OUTER


def rwkv_times_moe(nc, x_in, vec_in, wkT_in, wvT_in, wrT_in, woT_in, wrouT_in, wg_in, wu_in, wd_in, out):
    f32, i32 = mybir.dt.float32, mybir.dt.int32
    f16 = mybir.dt.float16
    ALU = mybir.AluOpType
    ACT = mybir.ActivationFunctionType
    X = mybir.AxisListType.X

    xn_rows = nc.dram_tensor("xn_rows", [TOK, D], f32, kind="Internal").ap()
    y_rows = nc.dram_tensor("y_rows", [ROWS, D], f32, kind="Internal").ap()

    x_v = x_in.rearrange("b (t p) d -> p b t d", p=P)
    out_order = lambda a: a.rearrange("b (t p) d -> p (b t) d", p=P)
    out_v = out_order(out)
    xn_v = xn_rows.rearrange("(b t p) d -> p b t d", p=P, t=TB)
    y_v = y_rows.rearrange("(s t p) d -> p t s d", p=P, t=T)

    ctx = ExitStack()
    with ctx:
        def sb(name, shape, dt=f32):
            return ctx.enter_context(nc.sbuf_tensor(name, shape, dt))

        def sem(name):
            return ctx.enter_context(nc.semaphore(name))

        wbig = sb("wbig", [P, 3 * C * E * D])
        wgu = wbig[:, 0:2 * C * E * D].rearrange("p (e c n) -> p e c n", c=C, e=E)
        wdn = wbig[:, 2 * C * E * D:].rearrange("p (c e n) -> p c e n", c=C, e=E)
        kT = sb("kT", [P, C, TOK])
        vT = sb("vT", [P, C, TOK])
        rT = sb("rT", [P, C, TOK])
        woT = sb("woT", [P, C, D])
        ident = sb("ident", [P, P])
        vec = sb("vec", [P, 5 * C])
        decay = sb("decay", [P, C])
        tok_idx = sb("tok_idx", [P, NT + 2], i32)
        dst_idx = sb("dst_idx", [P, NT], i32)
        tile_expert = sb("tile_expert", [1, NT], i32)
        used = sb("used", [1, 4], i32)
        slot_done = sb("slot_done", [1, 2 * (TOPK - 1)], i32)
        coef4 = sb("coef4", [P, T, TOPK])
        xg = sb("xg", [P, 2, 2, D])
        g_idx = sb("g_idx", [P, 2 * PAIRS], i32)
        s_idx = sb("s_idx", [P, 2 * PAIRS], i32)
        e_idx = sb("e_idx", [P, 6], i32)

        XNT = C * BATCH * (SEQ + 1)
        MIXN = C * SEQ
        arena = sb("arena", [P, XNT + 5 * MIXN + 3 * C * D])
        at = [0]

        def carve(n):
            at[0] += n
            return arena[:, at[0] - n:at[0]]

        xnT = carve(XNT).rearrange("p (c b s) -> p c b s", c=C, b=BATCH)
        diff = [carve(MIXN).rearrange("p (c s) -> p c s", c=C) for _ in range(2)]
        mix = [carve(MIXN).rearrange("p (c s) -> p c s", c=C) for _ in range(3)]
        wT = [carve(C * D).rearrange("p (c n) -> p c n", c=C) for _ in range(3)]
        at[0] = 0
        xTg = carve(2 * 2 * D).rearrange("p (b j c t) -> p b j c t", b=2, j=2, c=C)
        sg = carve(2 * 2 * D).rearrange("p (b j n) -> p b j n", b=2, j=2)
        hid = carve(2 * 2 * D).rearrange("p (b j n) -> p b j n", b=2, j=2)
        hT = carve(2 * 2 * D).rearrange("p (b j c t) -> p b j c t", b=2, j=2, c=C)
        ysb = carve(2 * 2 * D).rearrange("p (b j n) -> p b j n", b=2, j=2)
        mrun = carve(SEQ + 1)
        num = carve(SEQ + 1)
        den = carve(SEQ + 1)
        args = carve(4 * SEQ).rearrange("p (a s) -> p a s", a=4)
        ta = carve(SEQ)
        tb = carve(SEQ)
        wrou = sb("wrou", [P, C, E])
        lgT = [kT[0:E, c, (BATCH - 1) * SEQ:] for c in range(2)]
        x_sb = rT[:, :, :].rearrange("p c (t n) -> p (c t) n", n=D)

        EARLY, LATE = 18, 5
        wdn_flat = wbig[:, 2 * C * E * D:]
        scr_at, scr_end = [C * E * D - (EARLY + LATE) * D], [C * E * D - LATE * D]

        def scratch(*shape):
            n = 1
            for s in shape:
                n *= s
            v = wdn_flat[:, scr_at[0]:scr_at[0] + n]
            scr_at[0] += n
            assert scr_at[0] <= scr_end[0]
            if len(shape) == 1:
                return v
            names = "abc"[:len(shape)]
            return v.rearrange(f"p ({' '.join(names)}) -> p {' '.join(names)}", **dict(zip(names, shape)))

        stats = scratch(T, 6)
        mv = scratch(T, 2)
        veps, rstd, nbias = (scratch(T) for _ in range(3))
        mhalf = scratch(TB)
        rmax, rsum, rinv, cgt = (scratch(T) for _ in range(4))
        z, gt, eq, pre, keep = (scratch(T, E) for _ in range(5))
        pos = z
        totT, incl, excl, cmp = (scratch(E, T) for _ in range(4))
        ntile, tstart, ones16 = (scratch(E) for _ in range(3))
        m8 = scratch(T, 8)
        prod = scratch(T, TOPK * E)
        pos4 = scratch(T, TOPK)
        posi, ptilei, prowi = (scratch(T * TOPK).bitcast(i32) for _ in range(3))
        jrow = scratch(T)
        srow = scratch(TOPK)
        upper, ones = scratch(P), scratch(P)
        tdiag, tcol, ended = scratch(E)[0:E], scratch(1)[0:E], scratch(NT)[0:E]
        scr_at[0], scr_end[0] = C * E * D - LATE * D, C * E * D
        prob, sel, slot = (scratch(T, E) for _ in range(3))
        wsum, winv = (scratch(T) for _ in range(2))
        ptile, prow = (scratch(T, TOPK) for _ in range(2))
        val = scratch(2, T)
        iota_row = scratch(P)
        iota16 = scratch(P // 2).bitcast(f16)
        padv = scratch(1)
        padt = scratch(NT)
        endi, endp = scratch(TOPK)[0:1].bitcast(i32), scratch(2, TOPK - 1)[0:1].bitcast(i32)
        tend = scratch(E)
        dve_slots = lambda t: 2 + t % 2
        RING = 4
        ohA = sb("ohA", [P, RING, TOPK, NT], f16)
        ohB = sb("ohB", [P, RING, TOPK, P], f16)
        eqs = sb("eqs", [P, T, TOPK * E])
        late_prod = ohB[:, :, :, :].rearrange("p r s n -> p (r s n)").bitcast(f32).rearrange("p (t n) -> p t n", t=T)
        wsel = ohA[:, :, :, :].rearrange("p r s n -> p (r s n)").bitcast(f32)[:, 0:T * E].rearrange("p (t n) -> p t n", t=T)
        coef = ohA[:, :, :, :].rearrange("p r s n -> p (r s n)").bitcast(f32)[:, T * E:2 * T * E].rearrange("p (t n) -> p t n", t=T)
        signed, token, odd, high = (sb(name, [P, NT]) for name in ("signed", "token", "odd", "high"))

        y4 = wbig[:, 0:T * TOPK * D].rearrange("p (s t n) -> p t s n", t=T, s=TOPK)
        acc = wbig[:, T * TOPK * D:T * (TOPK + 1) * D].rearrange("p (t n) -> p t n", t=T)
        assert (TOPK - 1) * T * D <= (E - TOPK + 1) * 2 * C * D and T * TOPK * D <= 2 * C * E * D
        xre = [kT[:, n % C, (n // C) * SEQ:(n // C + 1) * SEQ].rearrange("p (t n) -> p t n", n=D) for n in range(T // 2)]

        ps = ctx.enter_context(nc.psum_tensor("ps", [P, 8, 512], f32))
        B_XT, B_G, B_HT, B_Y, B_R = 0, 1, 5, 6, 7
        XN_BANK = [(B_XT, B_Y), (B_HT, B_G + 3)]
        S_BANK = [B_G, B_G + 1, B_G + 2, B_G + 3, B_R, B_XT, B_HT, B_Y]
        FRONT, BACK = range(5), range(5, T // 2)
        logits = ps[:, B_R, 0:T * E].rearrange("p (t e) -> p t e", t=T)
        prefix = ps[:, B_Y, 0:T * E].rearrange("p (t e) -> p t e", t=T)
        totals = ps[:, B_Y, T * E:2 * T * E].rearrange("p (t e) -> p e t", t=T)
        table = [ps[:, B_HT, 0:NT], ps[:, B_XT, 0:NT]]

        x_in_s = [sem(f"x_in{b}") for b in range(BATCH)]
        small_in = sem("small_in")
        wgu_in, wdn_in = sem("wgu_in"), sem("wdn_in")
        xn_stored = sem("xn_stored")
        consts = sem("consts")
        N_CONSTS = 13
        var_ready, rstd_ready, nbias_ready = sem("var_ready"), sem("rstd_ready"), sem("nbias_ready")
        rmul_ready, rmix_ready = sem("rmul_ready"), sem("rmix_ready")
        vmul_ready, vmix_ready = sem("vmul_ready"), sem("vmix_ready")
        scaled_ready, half_ready, back_ready = sem("scaled_ready"), sem("half_ready"), sem("back_ready")
        xn_ready = [sem(f"xn_ready{b}") for b in range(BATCH)]
        xnt_psum, xnt_ready = sem("xnt_psum"), sem("xnt_ready")
        zcol = sem("zcol")
        diff_ready, mix_ready = sem("diff_ready"), sem("mix_ready")
        decay_ready = sem("decay_ready")
        proj_psum, proj_out = sem("proj_psum"), sem("proj_out")
        lgt_psum, lgt_ready = sem("lgt_psum"), sem("lgt_ready")
        logits_ready, z_ready, ez_ready = sem("logits_ready"), sem("z_ready"), sem("ez_ready")
        sel_ready, count_ready = sem("sel_ready"), sem("count_ready")
        digits_ready = sem("digits_ready")
        ohA_ready, ohB_ready, oh_used = sem("ohA_ready"), sem("ohB_ready"), sem("oh_used")
        slots_known, weights_ready = sem("slots_known"), sem("weights_ready")
        ended_ready, ended_psum, experts_ready = sem("ended_ready"), sem("ended_psum"), sem("experts_ready")
        index_ready, dst_ready = sem("index_ready"), sem("dst_ready")
        pool_turn = sem("pool_turn")
        gi_ready, si_ready, ei_ready = sem("gi_ready"), sem("si_ready"), sem("ei_ready")
        xg_in = [sem(f"xg_in{i}") for i in range(2)]
        y_out = [sem(f"y_out{i}") for i in range(2)]
        xt_psum, xt_ready = sem("xt_psum"), sem("xt_ready")
        gu_psum, sg_ready, h_ready = sem("gu_psum"), sem("sg_ready"), sem("h_ready")
        ht_psum, ht_ready = sem("ht_psum"), sem("ht_ready")
        y_psum, y_ready = sem("y_psum"), sem("y_ready")
        args_ready, exps_ready = sem("args_ready"), sem("exps_ready")
        wkv_ready = sem("wkv_ready")
        dve_step, pool_step = sem("dve_step"), sem("pool_step")
        y_in = [sem(f"y_in{i}") for i in range(TOPK - 1)]
        y_last_in = [sem(f"y_last_in{i}") for i in range(T // 2)]
        xre_in = sem("xre_in")
        acc_ready, silu_ready, s_psum, ffn_times_s, res_ready = (
            sem("acc_ready"), sem("silu_ready"), sem("s_psum"), sem("ffn_times_s"), sem("res_ready"))
        out_stored = sem("out_stored")

        def wait(eng, s, value):
            if not isinstance(value, int) or value > 0:
                eng.wait_ge(s, value)

        def pairs_used(eng):
            return (eng.value_load(used[0:1, 0:1], min_val=NEED // 2, max_val=NP // 2),
                    eng.value_load(used[0:1, 1:2], min_val=NEED - 3, max_val=NP - 3))

        def outer_steps(eng, step):
            step(0)
            with eng.Fori(1, OUTER - 1) as o:
                step(o)
            step(OUTER - 1)

        block = ctx.enter_context(nc.Block())

        @block.sync
        def _(sp):
            for b in range(BATCH):
                sp.dma_start(x_sb[:, b * TB:(b + 1) * TB, :], x_v[:, b]).then_inc(x_in_s[b], 16)
            for dst, src in ((vec[:, :], vec_in), (wrou[:, :, :], wrouT_in.rearrange("(c p) n -> p c n", p=P)),
                             (wT[0], wkT_in.rearrange("(c p) n -> p c n", p=P)),
                             (wT[1], wvT_in.rearrange("(c p) n -> p c n", p=P)),
                             (wT[2], wrT_in.rearrange("(c p) n -> p c n", p=P)),
                             (woT[:, :, :], woT_in.rearrange("(c p) n -> p c n", p=P))):
                sp.dma_start(dst, src).then_inc(small_in, 16)
            for b in range(BATCH):
                sp.wait_ge(xn_ready[b], 1)
                sp.dma_start(xn_v[:, b], x_sb[:, b * TB:(b + 1) * TB, :]).then_inc(xn_stored, 16)
            for half, src in ((0, wg_in), (1, wu_in)):
                for c in range(C):
                    sp.dma_start(wgu[:, :, c, half * D:(half + 1) * D],
                                 src.rearrange("e (c p) n -> c p e n", p=P)[c]).then_inc(wgu_in, 16)
            wd_v = wd_in.rearrange("e (c p) n -> c p e n", p=P)
            early_e = C * E - EARLY - LATE
            sp.dma_start(wdn[:, 0, 0:early_e], wd_v[0][:, 0:early_e]).then_inc(wdn_in, 16)
            sp.wait_ge(experts_ready, 1)
            sp.dma_start(wdn[:, 0, early_e:], wd_v[0][:, early_e:]).then_inc(wdn_in, 16)
            sp.dma_start(wdn[:, 1, 0:E - LATE], wd_v[1][:, 0:E - LATE]).then_inc(wdn_in, 16)
            sp.wait_ge(index_ready, 1)
            sp.wait_ge(slots_known, 3)
            sp.wait_ge(weights_ready, 1)
            sp.dma_start(wdn[:, 1, E - LATE:], wd_v[1][:, E - LATE:]).then_inc(wdn_in, 16)
            def reload(b):
                sp.wait_ge(wkv_ready, C * (b + 1))
                for n in range(C * b, C * (b + 1)):
                    sp.dma_start(xre[n], out_order(x_in)[:, 2 * n:2 * n + 2, :]).then_inc(xre_in, 16)

            for b in range(BATCH - 1):
                reload(b)
            counts = [sp.value_load(slot_done[0:1, n:n + 1], min_val=1, max_val=32 * (NP // 2))
                      for n in range(2 * (TOPK - 1))]
            pairs = sp.value_load(used[0:1, 2:3], min_val=NEED, max_val=NP)
            scattered = sp.value_load(used[0:1, 3:4], min_val=16 * NEED, max_val=16 * NP)
            for s in range(TOPK - 1):
                if s == TOPK - 2:
                    reload(BATCH - 1)
                for par in range(2):
                    sp.wait_ge(y_out[par], counts[2 * s + par])
                sp.dma_start(y4[:, :, s, :], y_v[:, :, s, :]).then_inc(y_in[s], 16)
            sp.wait_ge(y_psum, pairs)
            for i in range(2):
                sp.wait_ge(y_out[i], scattered)
            for n in range(T // 2):
                sp.dma_start(y4[:, 2 * n:2 * n + 2, TOPK - 1, :], y_v[:, 2 * n:2 * n + 2, TOPK - 1, :]).then_inc(y_last_in[n], 16)
            for n in range(T // 2):
                sp.wait_ge(res_ready, n + 1)
                sp.dma_start(out_v[:, 2 * n:2 * n + 2, :], acc[:, 2 * n:2 * n + 2, :]).then_inc(out_stored, 16)
            sp.wait_ge(out_stored, 16 * (T // 2))

        @block.gpsimd
        def _(pool):
            done = [0]

            def link(ins):
                done[0] += 1
                ins.then_inc(pool_step, 1)
                pool.wait_ge(pool_step, done[0])

            link(pool.memset(ident[:, :], 0.0))
            pool.affine_select(out=ident[:, :], in_=ident[:, :], compare_op=ALU.not_equal, fill=1.0,
                               base=0, pattern=[[-1, P]], channel_multiplier=1).then_inc(consts, 1)
            pool.memset(mhalf, -0.5).then_inc(consts, 1)
            link(pool.memset(keep, 1.0))
            pool.memset(keep[:, :, 0:1], 0.0).then_inc(consts, 1)
            pool.memset(ones, 1.0).then_inc(consts, 1)
            pool.memset(ones16, 1.0).then_inc(consts, 1)
            link(pool.memset(upper, 1.0))
            pool.affine_select(out=upper, in_=upper, compare_op=ALU.is_gt, fill=0.0,
                               base=0, pattern=[[1, P]], channel_multiplier=-1).then_inc(consts, 1)
            for dst, pattern, base, chan in ((iota_row, [[1, P]], 0, 0), (iota16, [[1, P]], 0, 0), (jrow, [[P, T]], 0, 0),
                                             (srow, [[1, TOPK]], 1, 0), (padv, [[1, 1]], ROWS + 1, 1),
                                             (val[:, 0, :], [[P, T]], 1, 1), (val[:, 1, :], [[-P, T]], -1, -1)):
                pool.iota(dst, pattern, base=base, channel_multiplier=chan,
                          allow_small_or_imprecise_dtypes=True).then_inc(consts, 1)
            pool.wait_ge(consts, N_CONSTS)
            for b in range(BATCH):
                t = slice(b * TB, (b + 1) * TB)
                pool.wait_ge(var_ready, b + 1)
                link(pool.tensor_scalar(veps[:, t], mv[:, t, 1], LN_EPS, None, ALU.add))
                pool.tensor_tensor(rstd[:, t], veps[:, t], mhalf, ALU.pow).then_inc(rstd_ready, 1)
            def token_diff(b):
                pool.wait_ge(xnt_ready, C * (b + 1))
                if b == 1:
                    pool.wait_ge(zcol, 1)
                    pool.wait_ge(diff_ready, 1)
                if b >= 2:
                    pool.wait_ge(mix_ready, b)
                    pool.wait_ge(rmul_ready, b - 1)
                pool.tensor_tensor(diff[b % 2], xnT[:, :, b, 1:SEQ + 1], xnT[:, :, b, 0:SEQ], ALU.subtract).then_inc(diff_ready, 1)

            def add_before(b, w):
                if w == 2:
                    pool.wait_ge(rmul_ready, b + 1)
                    pool.tensor_tensor(mix[2], mix[2], xnT[:, :, b, 0:SEQ], ALU.add).then_inc(rmix_ready, 1)
                else:
                    pool.wait_ge(vmul_ready, b)
                    pool.tensor_tensor(mix[1], mix[1], xnT[:, :, b, 0:SEQ], ALU.add).then_inc(vmix_ready, 1)

            token_diff(1)
            add_before(0, 2)
            token_diff(2)
            add_before(1, 1)
            add_before(1, 2)
            token_diff(3)
            add_before(2, 1)
            pool.wait_ge(digits_ready, 1)
            for t in range(T):
                if t == 2:
                    add_before(2, 2)
                if t == 12:
                    add_before(3, 1)
                if t >= RING:
                    pool.wait_ge(oh_used, t - RING + 1)
                for s in range(dve_slots(t), TOPK):
                    ins = pool.tensor_scalar(ohB[:, t % RING, s], iota_row, prow[:, t, s:s + 1], None, ALU.is_equal)
                ins.then_inc(ohB_ready, 1)
            add_before(3, 2)

            LAG = 4
            pool.wait_ge(index_ready, 1)
            pool.wait_ge(xn_stored, 16 * BATCH)

            def wait_alone(s, value):
                wait(pool, s, value)
                if not isinstance(value, int):
                    pool.sem_inc(pool_turn, 1)

            def indices(o, dst, src, landed, ready):
                for par in range(2):
                    wait_alone(landed[par], 16 * PAIRS * o)
                pool.tensor_copy(dst[:, :], src[:, bass.ds(2 * PAIRS * o, 2 * PAIRS)]).then_inc(ready, 1)
                wait_alone(ready, o + 1)

            def gather(i, par, idx, n):
                wait_alone(xt_psum, i - 1)
                for j in range(2):
                    pool.indirect_dma_start(out=xg[:, par, j, :], out_offset=None, in_=xn_rows,
                                            in_offset=bass.IndirectOffsetOnAxis(ap=idx[:, n + j:n + j + 1], axis=0)
                                            ).then_inc(xg_in[par], 16)

            def scatter(i, par, idx, n):
                wait_alone(y_ready, i + 1)
                for j in range(2):
                    pool.indirect_dma_start(out=y_rows, in_=ysb[:, par, j, :], in_offset=None,
                                            out_offset=bass.IndirectOffsetOnAxis(ap=idx[:, n + j:n + j + 1], axis=0),
                                            bounds_check=last_row, oob_is_err=False).then_inc(y_out[par], 16)

            last_row = pool.to_reg(ROWS - 1)

            def step(o):
                indices(o, g_idx, tok_idx, xg_in, gi_ready)
                for u in range(PAIRS):
                    gather(o * PAIRS + u, u % 2, g_idx, 2 * u)
                    if u == LAG:
                        if isinstance(o, int) and o == 0:
                            pool.wait_ge(dst_ready, 1)
                        indices(o, s_idx, dst_idx, y_out, si_ready)
                    if u >= LAG:
                        scatter(o * PAIRS + u - LAG, u % 2, s_idx, 2 * (u - LAG))
                    elif not isinstance(o, int) or o > 0:
                        scatter(o * PAIRS + u - LAG, u % 2, s_idx, 2 * (u - LAG + PAIRS))

            outer_steps(pool, step)
            pool.wait_ge(slots_known, 3)
            blocks, last3 = pairs_used(pool)
            gather(NEED, 0, tok_idx, 2 * NEED)
            scatter(NEED - LAG, 0, dst_idx, 2 * (NEED - LAG))
            for k in range(BLOCKS):
                with pool.If(blocks > NEED // 2 + k):
                    for i in (NEED + 2 * k + 1, NEED + 2 * k + 2):
                        gather(i, i % 2, tok_idx, 2 * i)
                        scatter(i - LAG, i % 2, dst_idx, 2 * (i - LAG))
            pool.tensor_copy(e_idx[:, :], dst_idx[:, bass.ds(2 * last3, 6)]).then_inc(ei_ready, 1)
            pool.wait_ge(ei_ready, 1)
            for n in range(3):
                scatter(last3 + n, (n + 1) % 2, e_idx, 2 * n)
            def add(n, a, b, ready):
                pool.tensor_tensor(acc[:, 2 * n:2 * n + 2, :], a, b, ALU.add).then_inc(ready, 1)

            for n in BACK:
                tt = slice(2 * n, 2 * n + 2)
                pool.wait_ge(scaled_ready, n - BACK[0] + 1)
                add(n, y4[:, tt, 0, :], y4[:, tt, 1, :], half_ready)
            for n in BACK:
                tt = slice(2 * n, 2 * n + 2)
                pool.wait_ge(half_ready, n - BACK[0] + 1)
                pool.wait_ge(scaled_ready, len(BACK) + n - BACK[0] + 1)
                add(n, acc[:, tt, :], y4[:, tt, 2, :], back_ready)
            pool.wait_ge(xre_in, 16 * (T // 2))
            for n in range(T // 2):
                pool.wait_ge(ffn_times_s, n + 1)
                add(n, acc[:, 2 * n:2 * n + 2, :], xre[n], res_ready)

        @block.scalar
        def _(act):
            def normalise(b):
                act.wait_ge(nbias_ready, b + 1)
                for t in range(b * TB, (b + 1) * TB):
                    ins = nc.scalar.activation(x_sb[:, t, :], x_sb[:, t, :], ACT.Identity,
                                               bias=nbias[:, t:t + 1], scale=rstd[:, t:t + 1])
                ins.then_inc(xn_ready[b], 1)

            def evac_xnt(b):
                for c in range(C):
                    act.wait_ge(xnt_psum, C * b + c + 1)
                    nc.scalar.copy(xnT[:, c, b, 1:SEQ + 1], ps[:, XN_BANK[b % 2][c], :]).then_inc(xnt_ready, 1)

            def scale_diff(b, w):
                act.wait_ge(diff_ready, b + 1)
                if b == 0:
                    act.wait_ge(small_in, 16 * 6)
                wait(act, proj_psum, ((b - 1) * 3 + w + 1) * C)
                for c in range(C):
                    ins = nc.scalar.activation(mix[w][:, c, :], diff[b % 2][:, c, :], ACT.Copy,
                                               scale=vec[:, (2 + w) * C + c:(2 + w) * C + c + 1])
                ins.then_inc(rmul_ready if w == 2 else vmul_ready, 1)

            def evac_lgt(b):
                act.wait_ge(lgt_psum, b + 1)
                wait(act, logits_ready, b - 1)
                nc.scalar.copy(lgT[b % 2], ps[0:E, B_G + b, :]).then_inc(lgt_ready, 1)

            normalise(0)
            normalise(1)
            evac_xnt(0)
            evac_xnt(1)
            evac_lgt(0)
            evac_xnt(2)
            evac_lgt(1)
            evac_xnt(3)
            evac_lgt(2)
            evac_lgt(3)
            scale_diff(0, 2)
            nc.scalar.activation(decay[:, :], vec[:, 0:C], ACT.Exp).then_inc(decay_ready, 1)
            act.wait_ge(z_ready, 1)
            nc.scalar.activation(prob, z, ACT.Exp).then_inc(ez_ready, 1)
            for b in range(BATCH):
                for w in range(3):
                    for c in range(C):
                        n = (b * 3 + w) * C + c
                        act.wait_ge(proj_psum, n + 1)
                        dst = (kT, vT, rT)[w][:, c, b * SEQ:(b + 1) * SEQ]
                        src = ps[:, B_G + n % 4, :]
                        if w == 2 and n < 3 * C:
                            act.wait_ge(xn_stored, 16 * BATCH)
                        if w == 2:
                            nc.scalar.activation(dst, src, ACT.Sigmoid).then_inc(proj_out, 1)
                        else:
                            nc.scalar.copy(dst, src).then_inc(proj_out, 1)
                    if b + 1 < BATCH and w > 0:
                        scale_diff(b + 1, w)

            def evac_x(i, par):
                act.wait_ge(xt_psum, i + 1)
                wait(act, gu_psum, i - 1)
                nc.scalar.copy(xTg[:, par].rearrange("p j c t -> p (j c t)"), ps[:, B_XT, :]).then_inc(xt_ready, 1)

            def silu(i, par):
                act.wait_ge(gu_psum, i + 1)
                wait(act, h_ready, i - 1)
                nc.scalar.activation(sg[:, par], ps[:, B_G + 2 * par:B_G + 2 * par + 2, 0:D], ACT.Silu).then_inc(sg_ready, 1)

            def evac_y(i, par, before):
                act.wait_ge(y_psum, i + 1)
                wait(act, y_out[par], 16 * before)
                nc.scalar.copy(ysb[:, par].rearrange("p j n -> p (j n)"), ps[:, B_Y, :]).then_inc(y_ready, 1)

            def step(o):
                first = isinstance(o, int) and o == 0
                for u in range(PAIRS):
                    i = o * PAIRS + u
                    evac_x(i + 1, (u + 1) % 2)
                    if u % HALF == 1:
                        piece = o * C + u // HALF
                        act.wait_ge(args_ready, piece + 1)
                        nc.scalar.activation(args, args, ACT.Exp).then_inc(exps_ready, 1)
                    silu(i, u % 2)
                    if u > 0 or not first:
                        evac_y(i - 1, (u - 1) % 2, i - 1 - (u - 1) % 2)

            evac_x(0, 0)
            outer_steps(act, step)
            blocks, last3 = pairs_used(act)
            for k in range(BLOCKS):
                with act.If(blocks > NEED // 2 + k):
                    for i in (NEED + 2 * k, NEED + 2 * k + 1):
                        evac_x(i + 1, (i + 1) % 2)
                        silu(i, i % 2)
                        evac_y(i - 1, (i - 1) % 2, i - 1 - (i - 1) % 2)
            evac_y(last3 + 2, 1, last3 + 1)
            act.wait_ge(y_in[0], 16)
            act.wait_ge(y_in[1], 16)
            for slots in ((0, 1), (2,)):
                if slots == (2,):
                    act.wait_ge(y_in[2], 16)
                for n in BACK:
                    for t in (2 * n, 2 * n + 1):
                        for k in slots:
                            ins = nc.scalar.activation(y4[:, t, k, :], y4[:, t, k, :], ACT.Copy, scale=coef4[:, t, k:k + 1])
                    ins.then_inc(scaled_ready, 1)
            for n in range(T // 2):
                act.wait_ge(acc_ready, n + 1)
                tt = slice(2 * n, 2 * n + 2)
                nc.scalar.activation(acc[:, tt, :], acc[:, tt, :], ACT.Silu).then_inc(silu_ready, 1)

        @block.tensor
        def _(pe):
            def product(dst, lhsT, rhs):
                for c in range(C):
                    ins = nc.tensor.matmul(dst, lhsT(c), rhs(c), start=(c == 0), stop=(c == C - 1))
                return ins

            def transpose_xn(b):
                pe.wait_ge(xn_ready[b], 1)
                for c in range(C):
                    wait(pe, xnt_ready, C * (b - 2) + c + 1)
                    for t in range(TB):
                        ins = nc.tensor.transpose(ps[:, XN_BANK[b % 2][c], t * P:(t + 1) * P],
                                                  x_sb[:, b * TB + t, c * P:(c + 1) * P], ident[:, :])
                    ins.then_inc(xnt_psum, 1)

            def route(b):
                pe.wait_ge(xnt_ready, C * (b + 1))
                product(ps[0:E, B_G + b, :], lambda c: wrou[:, c, :],
                        lambda c: xnT[:, c, b, 1:SEQ + 1]).then_inc(lgt_psum, 1)

            def transpose_logits(b):
                pe.wait_ge(lgt_ready, b + 1)
                for t in range(TB):
                    ins = nc.tensor.transpose(logits[:, b * TB + t, :], lgT[b % 2][:, t * P:(t + 1) * P], ident[0:E, 0:E])
                ins.then_inc(logits_ready, 1)

            pe.wait_ge(consts, N_CONSTS)
            transpose_xn(0)
            pe.wait_ge(small_in, 16 * 6)
            for b in range(1, BATCH):
                transpose_xn(b)
                if b >= 2:
                    transpose_logits(b - 2)
                route(b - 1)
            route(BATCH - 1)
            transpose_logits(BATCH - 2)
            transpose_logits(BATCH - 1)

            def project(b, between=lambda n: None):
                for w in range(3):
                    if w == 0 or b == 0 and w == 1:
                        pe.wait_ge(mix_ready, b + 1 + (w if b == 0 else 1))
                    elif w == 1:
                        pe.wait_ge(vmix_ready, b)
                    else:
                        pe.wait_ge(rmix_ready, b + 1)
                    for c in range(C):
                        n = (b * 3 + w) * C + c
                        wait(pe, proj_out, n - 3)
                        product(ps[:, B_G + n % 4, :], lambda h: wT[w][:, h, c * P:(c + 1) * P],
                                lambda h: mix[w][:, h, :]).then_inc(proj_psum, 1)
                        between(w * C + c)

            def count_rows(n):
                if n == 3:
                    pe.wait_ge(sel_ready, 1)
                    selr = sel.rearrange("p t e -> p (t e)")
                    nc.tensor.matmul(ps[:, B_Y, 0:T * E], upper, selr, start=True, stop=True)
                    nc.tensor.matmul(ps[:, B_Y, T * E:2 * T * E], ones, selr, start=True, stop=True).then_inc(count_ready, 1)

            def count_ended():
                pe.wait_ge(ended_ready, 1)
                nc.tensor.matmul(ps[0:1, B_R, 0:NT], ones[0:E, 0:1], ended, start=True, stop=True).then_inc(ended_psum, 1)

            placed = [0]

            def place_rows(tiles):
                for t in range(placed[0], placed[0] + tiles):
                    pe.wait_ge(ohA_ready, t + 1)
                    pe.wait_ge(ohB_ready, t + 1)
                    for s in range(TOPK):
                        ins = nc.tensor.matmul(table[s // 2], ohB[:, t % RING, s], ohA[:, t % RING, s],
                                               start=(t == 0 and s % 2 == 0), stop=(t == T - 1 and s % 2 == 1))
                    ins.then_inc(oh_used, 1)
                placed[0] += tiles

            project(0, count_rows)
            project(1)
            count_ended()
            project(2, lambda n: place_rows((0, 2, 2, 2, 2, 2)[n]))
            project(3, lambda n: place_rows((3, 3, 0, 0, 0, 0)[n]))
            assert placed[0] == T

            def transpose_x(i, par):
                pe.wait_ge(xg_in[par], 16 * (i - par + 2))
                wait(pe, xt_ready, i)
                for j in range(2):
                    for c in range(C):
                        ins = nc.tensor.transpose(ps[:, B_XT, (j * C + c) * P:(j * C + c + 1) * P],
                                                  xg[:, par, j, c * P:(c + 1) * P], ident[:, :])
                ins.then_inc(xt_psum, 1)

            def gate_up(par, j, expert):
                return product(ps[:, B_G + 2 * par + j, :], lambda c: xTg[:, par, j, c, :],
                               lambda c: wgu[:, bass.ds(expert, 1), c, :].rearrange("p a n -> p (a n)"))

            def transpose_h(i, par):
                pe.wait_ge(h_ready, i + 1)
                wait(pe, ht_ready, i)
                for j in range(2):
                    for c in range(C):
                        ins = nc.tensor.transpose(ps[:, B_HT, (j * C + c) * P:(j * C + c + 1) * P],
                                                  hid[:, par, j, c * P:(c + 1) * P], ident[:, :])
                ins.then_inc(ht_psum, 1)

            def down(i, par, experts):
                pe.wait_ge(ht_ready, i + 1)
                wait(pe, y_ready, i)
                for j in range(2):
                    ins = product(ps[:, B_Y, j * D:(j + 1) * D], lambda c: hT[:, par, j, c, :],
                                  lambda c: wdn[:, c, bass.ds(experts[j], 1), :].rearrange("p a n -> p (a n)"))
                ins.then_inc(y_psum, 1)

            def experts_of(i):
                return [pe.value_load(tile_expert[0:1, bass.ds(2 * i + j, 1)], min_val=0, max_val=E - 1) for j in range(2)]

            def pair(i, par, first=None):
                if not first:
                    transpose_x(i + 1, 1 - par)
                now = first or experts_of(i)
                pe.wait_ge(xt_ready, i + 1)
                wait(pe, h_ready, i - 1)
                gate_up(par, 0, now[0])
                if first:
                    transpose_x(i + 1, 1 - par)
                else:
                    before = experts_of(i - 1)
                    transpose_h(i - 1, 1 - par)
                gate_up(par, 1, now[1]).then_inc(gu_psum, 1)
                if not first:
                    down(i - 1, 1 - par, before)

            def step(o):
                first = isinstance(o, int) and o == 0
                for u in range(PAIRS):
                    if first and u == 1:
                        pe.wait_ge(wdn_in, 16 * 4)
                    pair(o * PAIRS + u, u % 2, first_experts if first and u == 0 else None)

            pe.wait_ge(experts_ready, 1)
            first_experts = experts_of(0)
            transpose_x(0, 0)
            pe.wait_ge(wgu_in, 16 * 4)
            pe.wait_ge(proj_out, BATCH * 3 * C)
            outer_steps(pe, step)
            blocks, last3 = pairs_used(pe)
            for k in range(BLOCKS):
                with pe.If(blocks > NEED // 2 + k):
                    for i in (NEED + 2 * k, NEED + 2 * k + 1):
                        pair(i, i % 2)
            last = experts_of(last3 + 2)
            transpose_h(last3 + 2, 1)
            down(last3 + 2, 1, last)
            pe.wait_ge(wkv_ready, C * BATCH)
            for n in range(T // 2):
                if S_BANK[n] == B_XT:
                    pe.wait_ge(xt_ready, last3 + 4)
                elif S_BANK[n] == B_HT:
                    pe.wait_ge(ht_ready, last3 + 3)
                elif S_BANK[n] == B_Y:
                    pe.wait_ge(y_ready, last3 + 3)
                for j in range(2):
                    t = 2 * n + j
                    ins = product(ps[:, S_BANK[n], j * D:(j + 1) * D], lambda c: rT[:, c, t * P:(t + 1) * P],
                                  lambda c: woT[:, c, :])
                ins.then_inc(s_psum, 1)

        @block.vector
        def _(dve):
            V = nc.vector
            base, done = [0], [0]

            def link(ins):
                done[0] += 1
                ins.then_inc(dve_step, 1)
                dve.wait_ge(dve_step, base[0] + done[0])

            def inner(a, n=E):
                return a.unsqueeze(2).to_broadcast([a.shape[0], a.shape[1], n])

            V.memset(xnT[:, :, :, 0:1], 0.0).then_inc(zcol, 1)
            for b in range(BATCH + 1):
                if b < BATCH:
                    dve.wait_ge(x_in_s[b], 16)
                    for t in range(b * TB, (b + 1) * TB):
                        ins = V.bn_stats(stats[:, t, :], x_sb[:, t, :])
                    link(ins)
                    for t in range(b * TB, (b + 1) * TB):
                        ins = V.bn_aggr(mv[:, t, :], stats[:, t, :])
                    ins.then_inc(var_ready, 1)
                if 0 < b <= 2:
                    t = slice((b - 1) * TB, b * TB)
                    dve.wait_ge(rstd_ready, b)
                    dve.wait_ge(var_ready, b)
                    V.scalar_tensor_tensor(out=nbias[:, t], in0=mv[:, t, 0], scalar=-1.0, in1=rstd[:, t],
                                           op0=ALU.mult, op1=ALU.mult).then_inc(nbias_ready, 1)
            for b in (2, 3):
                dve.wait_ge(var_ready, b + 1)
                dve.wait_ge(rstd_ready, b + 1)
                for t in range(b * TB, (b + 1) * TB):
                    ins = V.tensor_scalar(x_sb[:, t, :], x_sb[:, t, :], mv[:, t, 0:1], rstd[:, t:t + 1],
                                          ALU.subtract, ALU.mult)
                ins.then_inc(xn_ready[b], 1)
            dve.wait_ge(xnt_ready, C)
            dve.wait_ge(zcol, 1)
            V.tensor_tensor(diff[0], xnT[:, :, 0, 1:SEQ + 1], xnT[:, :, 0, 0:SEQ], ALU.subtract).then_inc(diff_ready, 1)

            def mixes(b):
                dve.wait_ge(diff_ready, b + 1)
                if b == 0:
                    dve.wait_ge(small_in, 16 * 6)
                for w in range(2 if b == 0 else 1):
                    wait(dve, proj_psum, ((b - 1) * 3 + w + 1) * C)
                    for c in range(C):
                        m = vec[:, (2 + w) * C + c:(2 + w) * C + c + 1]
                        ins = V.scalar_tensor_tensor(out=mix[w][:, c, :], in0=diff[b % 2][:, c, :], scalar=m,
                                                     in1=xnT[:, c, b, 0:SEQ], op0=ALU.mult, op1=ALU.add)
                    ins.then_inc(mix_ready, 1)

            mixes(0)
            dve.wait_ge(logits_ready, BATCH)
            link(V.tensor_reduce(rmax, logits, X, ALU.max))
            V.tensor_tensor(z, logits, inner(rmax), ALU.subtract).then_inc(z_ready, 1)
            dve.wait_ge(ez_ready, 1)
            link(V.tensor_reduce(rsum, prob, X, ALU.add))
            link(V.reciprocal(rinv, rsum))
            link(V.tensor_tensor(prob, prob, inner(rinv), ALU.mult))
            for t in range(T):
                ins = V.max(m8[:, t, :], prob[:, t, :])
            link(ins)
            kth = m8[:, :, TOPK - 1]
            dve.wait_ge(consts, N_CONSTS)
            V.tensor_tensor(gt, prob, inner(kth), ALU.is_gt)
            link(V.tensor_tensor(eq, prob, inner(kth), ALU.is_equal))
            V.tensor_reduce(cgt, gt, X, ALU.add)
            flat = lambda a: a.rearrange("p a b -> p (a b)")
            link(V.tensor_tensor_scan(flat(pre), flat(keep), flat(eq), 0.0, ALU.mult, ALU.add))
            link(V.tensor_tensor(pre, pre, inner(cgt), ALU.add))
            link(V.scalar_tensor_tensor(out=eq, in0=pre, scalar=float(TOPK), in1=eq, op0=ALU.is_le, op1=ALU.mult))
            V.tensor_tensor(sel, gt, eq, ALU.add).then_inc(sel_ready, 1)
            dve.wait_ge(sel_ready, 1)
            link(V.tensor_tensor_scan(flat(slot), flat(keep), flat(sel), 0.0, ALU.mult, ALU.add))
            link(V.tensor_tensor(slot, slot, sel, ALU.mult))
            dve.wait_ge(decay_ready, 1)
            V.tensor_scalar(decay[:, :], decay[:, :], -1.0, None, ALU.mult)
            mixes(1)
            dve.wait_ge(count_ready, 1)
            link(V.tensor_copy(totT, totals))
            link(V.tensor_tensor_scan(flat(incl), flat(keep), flat(totT), 0.0, ALU.mult, ALU.add))
            V.tensor_tensor(excl, incl, totT, ALU.subtract)
            link(V.tensor_tensor(cmp, inner(incl[:, :, T - 1], T), jrow.unsqueeze(1).to_broadcast([P, E, T]), ALU.is_gt))
            link(V.tensor_reduce(ntile, cmp, X, ALU.add))
            link(V.tensor_tensor_scan(tend, ones16, ntile, 0.0, ALU.mult, ALU.add))
            link(V.tensor_tensor(tstart, tend, ntile, ALU.subtract))
            link(V.scalar_tensor_tensor(out=excl, in0=inner(tstart, T), scalar=float(P), in1=excl, op0=ALU.mult, op1=ALU.add))
            link(V.tensor_tensor(pos, prefix, excl.rearrange("p e t -> p t e"), ALU.add))
            eq4 = eqs.rearrange("p t (s e) -> p t s e", s=TOPK)
            pr4 = prod.rearrange("p t (s e) -> p t s e", s=TOPK)
            by_slot = lambda a: a.unsqueeze(2).to_broadcast([P, T, TOPK, E])
            link(V.tensor_tensor(eq4, by_slot(slot), srow.unsqueeze(1).unsqueeze(3).to_broadcast([P, T, TOPK, E]), ALU.is_equal))
            link(V.tensor_tensor(pr4, eq4, by_slot(pos), ALU.mult))
            link(V.tensor_reduce(pos4, pr4, X, ALU.add))
            link(V.tensor_copy(posi, flat(pos4)))
            V.tensor_scalar(ptilei, posi, 7, None, ALU.logical_shift_right)
            link(V.tensor_scalar(prowi, posi, P - 1, None, ALU.bitwise_and))
            V.tensor_copy(flat(ptile), ptilei)
            V.tensor_copy(flat(prow), prowi).then_inc(digits_ready, 1)

            def row_weights():
                link(V.tensor_tensor(wsel, prob, sel, ALU.mult))
                link(V.tensor_reduce(wsum, wsel, X, ALU.add))
                link(V.reciprocal(winv, wsum))
                link(V.tensor_tensor(coef, wsel, inner(winv), ALU.mult))
                late4 = late_prod.rearrange("p t (s e) -> p t s e", s=TOPK)
                link(V.tensor_tensor(late4, eq4, by_slot(coef), ALU.mult))
                V.tensor_reduce(coef4[:, :, :], late4, X, ALU.add).then_inc(weights_ready, 1)

            def ended_before():
                link(V.tensor_tensor(tdiag, tend[0:E, :], ident[0:E, 0:E], ALU.mult))
                link(V.tensor_reduce(tcol, tdiag, X, ALU.add))
                V.tensor_scalar(ended, iota_row[0:E, 0:NT], tcol, None, ALU.is_ge).then_inc(ended_ready, 1)

            def slots_done():
                link(V.tensor_copy(endi, tend[0:1, E - TOPK:E]))
                link(V.tensor_scalar(used[:, 0:1], endi[:, TOPK - 1:TOPK], 3, None, ALU.add))
                link(V.tensor_scalar(used[:, 0:1], used[:, 0:1], 2, None, ALU.logical_shift_right))
                link(V.tensor_scalar(used[:, 2:3], used[:, 0:1], 1, None, ALU.logical_shift_left))
                V.tensor_scalar(used[:, 1:2], used[:, 2:3], -3, None, ALU.add)
                V.tensor_scalar(used[:, 3:4], used[:, 2:3], 4, None, ALU.logical_shift_left).then_inc(slots_known, 1)
                for par, more in ((0, 3), (1, 1)):
                    link(V.tensor_scalar(endp[:, par, :], endi[:, 0:TOPK - 1], more, None, ALU.add))
                    link(V.tensor_scalar(endp[:, par, :], endp[:, par, :], 2, None, ALU.logical_shift_right))
                    V.tensor_scalar(slot_done.rearrange("p (s a) -> p a s", a=2)[:, par, :], endp[:, par, :], 5, None,
                                    ALU.logical_shift_left).then_inc(slots_known, 1)

            def expert_of_tiles():
                dve.wait_ge(ended_psum, 1)
                V.tensor_scalar(tile_expert[:, :], ps[0:1, B_R, 0:NT], float(E - 1), None, ALU.min).then_inc(experts_ready, 1)

            ended_before()
            mixes(2)
            dve.wait_ge(digits_ready, 1)
            for t in range(T):
                if t == T // 2 + 1:
                    expert_of_tiles()
                if t == T // 2:
                    mixes(3)
                if t >= RING:
                    dve.wait_ge(oh_used, t - RING + 1)
                for s in range(dve_slots(t)):
                    V.tensor_scalar(ohB[:, t % RING, s], iota16, prow[:, t, s:s + 1], None, ALU.is_equal)
                for s in range(TOPK):
                    ins = V.tensor_scalar(ohA[:, t % RING, s], iota16[:, 0:NT], ptile[:, t, s:s + 1], val[:, s % 2, t:t + 1],
                                          ALU.is_equal, ALU.mult)
                ins.then_inc(ohA_ready, 1)
            dve.wait_ge(oh_used, T)
            V.memset(tok_idx[:, NT:], 0)
            V.tensor_scalar(high[:, :], table[1], 0.0, float(2 * TOK), ALU.not_equal, ALU.mult)
            link(V.tensor_copy(signed[:, :], table[0]))
            link(V.tensor_tensor(signed[:, :], signed[:, :], table[1], ALU.add))
            V.tensor_scalar(padt, signed[:, :], 0.0, padv, ALU.is_equal, ALU.mult)
            link(V.scalar_tensor_tensor(out=token[:, :], in0=signed[:, :], scalar=-1.0, in1=signed[:, :], op0=ALU.mult, op1=ALU.max))
            link(V.scalar_tensor_tensor(out=dst_idx[:, :], in0=token[:, :], scalar=-1.0, in1=padt, op0=ALU.add, op1=ALU.add))
            V.tensor_scalar(tok_idx[:, 0:NT], dst_idx[:, :], TOK - 1, None, ALU.bitwise_and).then_inc(index_ready, 1)
            V.tensor_copy(token[:, :], dst_idx[:, :])
            link(V.tensor_scalar(odd[:, :], signed[:, :], 0.0, float(TOK), ALU.is_lt, ALU.mult))
            link(V.tensor_tensor(token[:, :], token[:, :], odd[:, :], ALU.add))
            V.tensor_tensor(dst_idx[:, :], token[:, :], high[:, :], ALU.add).then_inc(dst_ready, 1)
            slots_done()
            row_weights()
            dve.wait_ge(rmix_ready, BATCH)

            def evac_h(i, par):
                dve.wait_ge(ht_psum, i + 1)
                wait(dve, y_psum, i - 1)
                V.tensor_copy(hT[:, par].rearrange("p j c t -> p (j c t)"), ps[:, B_HT, :]).then_inc(ht_ready, 1)

            def hidden(i, par):
                dve.wait_ge(sg_ready, i + 1)
                wait(dve, ht_psum, i - 1)
                V.tensor_tensor(hid[:, par], sg[:, par], ps[:, B_G + 2 * par:B_G + 2 * par + 2, D:2 * D], ALU.mult).then_inc(h_ready, 1)

            def wkv(o, c, part):
                piece = o * C + c
                cols = bass.ds(o * SEQ, SEQ)
                k, v, r = kT[:, c, cols], vT[:, c, cols], rT[:, c, cols]
                w, first = decay[:, c:c + 1], vec[:, C + c:C + c + 1]
                m_old, m_new = mrun[:, 0:SEQ], mrun[:, 1:SEQ + 1]
                e_keep, e_new, o_keep, o_new = (args[:, a, :] for a in range(4))
                H = SEQ // 2
                if part == 0:
                    V.memset(mrun[:, 0:1], NEG_INF)
                    V.memset(num[:, 0:1], 0.0)
                    V.memset(den[:, 0:1], 0.0)
                    link(V.tensor_tensor_scan(m_new, w.to_broadcast([P, SEQ]), k, NEG_INF, ALU.add, ALU.max))
                elif part == 1:
                    V.scalar_tensor_tensor(out=e_keep, in0=m_old, scalar=w, in1=m_new, op0=ALU.add, op1=ALU.subtract)
                    V.tensor_tensor(e_new, k, m_new, ALU.subtract)
                    link(V.scalar_tensor_tensor(out=ta, in0=k, scalar=first, in1=m_old, op0=ALU.add, op1=ALU.max))
                elif part == 2:
                    V.tensor_tensor(o_keep, m_old, ta, ALU.subtract)
                    V.scalar_tensor_tensor(out=o_new, in0=k, scalar=first, in1=ta, op0=ALU.add,
                                           op1=ALU.subtract).then_inc(args_ready, 1)
                elif part == 3:
                    dve.wait_ge(exps_ready, piece + 1)
                    link(V.tensor_tensor(tb, e_new, v, ALU.mult))
                    link(V.tensor_tensor_scan(num[:, 1:SEQ + 1], e_keep, tb, 0.0, ALU.mult, ALU.add))
                elif part == 4:
                    V.tensor_tensor_scan(den[:, 1:SEQ + 1], e_keep, e_new, 0.0, ALU.mult, ALU.add)
                    V.tensor_tensor(ta, o_new, v, ALU.mult)
                    link(V.tensor_tensor(tb, o_keep, num[:, 0:SEQ], ALU.mult))
                elif part == 5:
                    V.tensor_tensor(ta, ta, tb, ALU.add)
                    link(V.tensor_tensor(o_keep, o_keep, den[:, 0:SEQ], ALU.mult))
                elif part == 6:
                    link(V.tensor_tensor(o_keep, o_keep, o_new, ALU.add))
                elif part == 7:
                    V.reciprocal(o_keep[:, 0:H], o_keep[:, 0:H])
                elif part == 8:
                    link(V.reciprocal(o_keep[:, H:SEQ], o_keep[:, H:SEQ]))
                elif part == 9:
                    link(V.tensor_tensor(ta, ta, o_keep, ALU.mult))
                    V.tensor_tensor(r, ta, r, ALU.mult).then_inc(wkv_ready, 1)
                    dve.wait_ge(wkv_ready, piece + 1)

            PARTS = (((0,), (1, 2)), ((), (3,)), ((4,), (5, 6)), ((7,), (8, 9)))

            def step(o):
                first = isinstance(o, int) and o == 0
                for u in range(PAIRS):
                    i = o * PAIRS + u
                    if u > 0 or not first:
                        evac_h(i - 1, (u - 1) % 2)
                    for part in PARTS[u % HALF][0]:
                        wkv(o, u // HALF, part)
                    hidden(i, u % 2)
                    for part in PARTS[u % HALF][1]:
                        wkv(o, u // HALF, part)

            start = done[0]
            step(0)
            per_step = done[0] - start
            with dve.Fori(1, OUTER - 1) as o:
                done[0] = start
                base[0] = o * per_step
                step(o)
                assert done[0] == start + per_step
            base[0], done[0] = (OUTER - 1) * per_step, start
            step(OUTER - 1)
            blocks, last3 = pairs_used(dve)
            for k in range(BLOCKS):
                with dve.If(blocks > NEED // 2 + k):
                    for i in (NEED + 2 * k, NEED + 2 * k + 1):
                        evac_h(i - 1, (i - 1) % 2)
                        hidden(i, i % 2)
            evac_h(last3 + 2, 1)
            def weighted(n, k):
                for t in (2 * n, 2 * n + 1):
                    if k == 0:
                        ins = V.tensor_scalar(acc[:, t, :], y4[:, t, 0, :], coef4[:, t, 0:1], None, ALU.mult)
                    else:
                        ins = V.scalar_tensor_tensor(out=acc[:, t, :], in0=y4[:, t, k, :], scalar=coef4[:, t, k:k + 1],
                                                     in1=acc[:, t, :], op0=ALU.mult, op1=ALU.add)
                return ins

            for k in range(TOPK - 1):
                dve.wait_ge(y_in[k], 16)
                for n in FRONT:
                    ins = weighted(n, k)
                link(ins)

            def gated(n):
                tt = slice(2 * n, 2 * n + 2)
                dve.wait_ge(silu_ready, n + 1)
                dve.wait_ge(s_psum, n + 1)
                V.tensor_tensor(acc[:, tt, :], acc[:, tt, :], ps[:, S_BANK[n], :].rearrange("p (t n) -> p t n", t=2),
                                ALU.mult).then_inc(ffn_times_s, 1)

            for n in range(T // 2):
                dve.wait_ge(y_last_in[n], 16)
                if n in BACK:
                    dve.wait_ge(back_ready, n - BACK[0] + 1)
                weighted(n, TOPK - 1).then_inc(acc_ready, 1)
                if n > 0:
                    gated(n - 1)
            gated(T // 2 - 1)


def kernel(**inputs):
    import numpy as np
    import concourse.bacc as bacc
    from concourse.bass_utils import run_bass_kernel_spmd

    a = {k.replace("L0_", ""): np.asarray(v) for k, v in inputs.items()}
    vecs = np.stack([a["attn_time_decay"], a["attn_time_first"], a["attn_time_mix_key"].reshape(-1),
                     a["attn_time_mix_value"].reshape(-1), a["attn_time_mix_receptance"].reshape(-1)])
    arrays = {
        "x_in": a["attn_hidden"],
        "vec_in": vecs.reshape(5, C, P).transpose(2, 0, 1).reshape(P, 5 * C),
        "wkT_in": a["attn_Wk"].T, "wvT_in": a["attn_Wv"].T, "wrT_in": a["attn_Wr"].T, "woT_in": a["attn_Wo"].T,
        "wrouT_in": a["ffn_w_router"].T,
        "wg_in": a["ffn_w_gate"], "wu_in": a["ffn_w_up"], "wd_in": a["ffn_w_down"],
    }
    arrays = {k: np.ascontiguousarray(v) for k, v in arrays.items()}
    nc = bacc.Bacc("TRN2", target_bir_lowering=False, num_devices=1)
    args = [nc.dram_tensor(k, v.shape, mybir.dt.from_np(v.dtype), kind="ExternalInput").ap() for k, v in arrays.items()]
    out = nc.dram_tensor("out", arrays["x_in"].shape, mybir.dt.float32, kind="ExternalOutput").ap()
    rwkv_times_moe(nc, *args, out)
    r = run_bass_kernel_spmd(nc, [arrays], core_ids=[0])
    return r.results[0]["out"]
```
